# Optimizing a Trainium2 kernel written in Bass

```python
import numpy as np
import jax
import jax.numpy as jnp

def _softmax(x, axis=-1):
    return jax.nn.softmax(x, axis=axis)

def _gelu(x):
    return jax.nn.gelu(x, approximate=True)

def _silu(x):
    return jax.nn.silu(x)

def _sigmoid(x):
    return jax.nn.sigmoid(x)

def _layernorm(x, axis=-1, eps=1e-05):
    m = jnp.mean(x, axis=axis, keepdims=True)
    v = jnp.var(x, axis=axis, keepdims=True)
    return (x - m) / jnp.sqrt(v + eps)

def _scatter_add(tgt, idx, src, axis=0):
    return tgt.at[idx].add(src)

def _segment_sum(src, seg, n):
    return jax.ops.segment_sum(src, seg, n)
kernel_name = 'mk_gnn_ffn_d1_gnn_r8_f16b9f'

def setup_inputs(seed: int=0):
    np.random.seed(seed)
    _w = jnp.asarray

    def _rec_inputs():
        import jax
        import jax.numpy as jnp
        _gk = jax.random.key(seed)
        x = -0.0003713 + 1 * jax.random.normal(jax.random.fold_in(_gk, 1), (6250, 256), jnp.float32)
        src = jax.random.randint(jax.random.fold_in(_gk, 2), (100000,), 0, 6250, jnp.int32)
        dst = jnp.minimum((6250 * jax.random.uniform(jax.random.fold_in(_gk, 3), (100000,)) ** 2.0).astype(jnp.int32), 49999)
        _o = jnp.argsort(dst, stable=True)
        src = src[_o]
        dst = dst[_o]
        edge_weight1 = 0.000937891 + 0.999965 * jax.random.normal(jax.random.fold_in(_gk, 13), (100000, 1), jnp.float32)
        return (x, src, dst, edge_weight1)
    x, src, dst, edge_weight1 = _rec_inputs()

    def _L0_gnn_setup():
        import jax, jax.numpy as jnp
        import numpy as np
        N, E, IN_DIM, HEADS, OUT_DIM, N_GRAPHS = (6250, 100000, 256, 4, 64, 8)
        HC = HEADS * OUT_DIM
        NEG_SLOPE = 0.2
        LN_EPS = 1e-05
        key = jax.random.key(seed)
        ks = jax.random.split(key, 12)
        x = jax.random.normal(ks[0], (N, IN_DIM), jnp.float32)
        edge_attr = jax.random.normal(ks[1], (E, 1), jnp.float32)
        src = jax.random.randint(ks[2], (E,), 0, N, dtype=jnp.int32)
        dst = jax.random.randint(ks[3], (E,), 0, N, dtype=jnp.int32)
        edge_index = jnp.stack([src, dst]).astype(jnp.int64)
        batch = jnp.sort(jax.random.randint(ks[4], (N,), 0, N_GRAPHS, dtype=jnp.int32)).astype(jnp.int64)
        s = 1.0 / np.sqrt(IN_DIM)
        W_src = jax.random.uniform(ks[5], (IN_DIM, HC), jnp.float32, -s, s)
        W_dst = jax.random.uniform(ks[6], (IN_DIM, HC), jnp.float32, -s, s)
        att_src = jax.random.uniform(ks[7], (HEADS, OUT_DIM), jnp.float32, -s, s)
        att_dst = jax.random.uniform(ks[8], (HEADS, OUT_DIM), jnp.float32, -s, s)
        bias = jnp.zeros((HC,), jnp.float32)
        ln_gamma = jnp.ones((HC,), jnp.float32)
        ln_beta = jnp.zeros((HC,), jnp.float32)
        prelu_w = jnp.full((HC,), 0.25, jnp.float32)
        return {'x': x, 'edge_attr': edge_attr, 'W_src': W_src, 'W_dst': W_dst, 'att_src': att_src, 'att_dst': att_dst, 'bias': bias, 'ln_gamma': ln_gamma, 'ln_beta': ln_beta, 'prelu_w': prelu_w, 'edge_index': edge_index, 'batch': batch}
    _L0_gnn_all = _L0_gnn_setup()
    _L0_gnn_in = {k: v for k, v in _L0_gnn_all.items() if k in ('W_src', 'W_dst', 'att_src', 'att_dst', 'bias', 'ln_gamma', 'ln_beta', 'prelu_w')}
    del _L0_gnn_all

    def _L0_ffn_setup():
        import jax, jax.numpy as jnp
        import numpy as np
        D_MODEL = 256
        EXPERT_DIM = 512
        NUM_EXPERTS = 8
        TOP_K = 2
        SEQ_LEN = 256
        BATCH = 2
        key = jax.random.key(seed)
        ks = jax.random.split(key, 8)
        s = 0.02
        x = jax.random.normal(ks[0], (SEQ_LEN, BATCH, D_MODEL), dtype=jnp.float32)
        Wg = jax.random.normal(ks[1], (D_MODEL, NUM_EXPERTS), dtype=jnp.float32) * s
        bg = jax.random.normal(ks[2], (NUM_EXPERTS,), dtype=jnp.float32) * s
        bias = jnp.zeros((NUM_EXPERTS,), dtype=jnp.float32)
        W1 = jax.random.normal(ks[3], (NUM_EXPERTS, D_MODEL, EXPERT_DIM), dtype=jnp.float32) * s
        b1 = jax.random.normal(ks[4], (NUM_EXPERTS, EXPERT_DIM), dtype=jnp.float32) * s
        W2 = jax.random.normal(ks[5], (NUM_EXPERTS, EXPERT_DIM, D_MODEL), dtype=jnp.float32) * s
        b2 = jax.random.normal(ks[6], (NUM_EXPERTS, D_MODEL), dtype=jnp.float32) * s
        return {'x': x, 'Wg': Wg, 'bg': bg, 'bias': bias, 'W1': W1, 'b1': b1, 'W2': W2, 'b2': b2}
    _L0_ffn_all = _L0_ffn_setup()
    _L0_ffn_in = {k: v for k, v in _L0_ffn_all.items() if k in ('Wg', 'bg', 'bias', 'W1', 'b1', 'W2', 'b2')}
    del _L0_ffn_all
    return {'x': x, 'src': src, 'dst': dst, 'edge_weight1': edge_weight1, 'L0_gnn_W_src': _L0_gnn_in['W_src'], 'L0_gnn_W_dst': _L0_gnn_in['W_dst'], 'L0_gnn_att_src': _L0_gnn_in['att_src'], 'L0_gnn_att_dst': _L0_gnn_in['att_dst'], 'L0_gnn_bias': _L0_gnn_in['bias'], 'L0_gnn_ln_gamma': _L0_gnn_in['ln_gamma'], 'L0_gnn_ln_beta': _L0_gnn_in['ln_beta'], 'L0_gnn_prelu_w': _L0_gnn_in['prelu_w'], 'L0_ffn_Wg': _L0_ffn_in['Wg'], 'L0_ffn_bg': _L0_ffn_in['bg'], 'L0_ffn_bias': _L0_ffn_in['bias'], 'L0_ffn_W1': _L0_ffn_in['W1'], 'L0_ffn_b1': _L0_ffn_in['b1'], 'L0_ffn_W2': _L0_ffn_in['W2'], 'L0_ffn_b2': _L0_ffn_in['b2']}

def reference(x, src, dst, edge_weight1, L0_gnn_W_src, L0_gnn_W_dst, L0_gnn_att_src, L0_gnn_att_dst, L0_gnn_bias, L0_gnn_ln_gamma, L0_gnn_ln_beta, L0_gnn_prelu_w, L0_ffn_Wg, L0_ffn_bg, L0_ffn_bias, L0_ffn_W1, L0_ffn_b1, L0_ffn_W2, L0_ffn_b2):
    import jax
    import jax.numpy as jnp

    def _L0_gnn_ref(x, edge_attr, W_src, W_dst, att_src, att_dst, bias, ln_gamma, ln_beta, prelu_w, edge_index, batch):
        import jax, jax.numpy as jnp
        import numpy as np
        N, E, IN_DIM, HEADS, OUT_DIM, N_GRAPHS = (6250, 100000, 256, 4, 64, 8)
        HC = HEADS * OUT_DIM
        NEG_SLOPE = 0.2
        LN_EPS = 1e-05
        src, dst = (edge_index[0], edge_index[1])
        n = x.shape[0]
        h_src = (x @ W_src).reshape(n, HEADS, OUT_DIM)
        h_dst = (x @ W_dst).reshape(n, HEADS, OUT_DIM)
        a_src = jnp.einsum('nhc,hc->nh', h_src, att_src)
        a_dst = jnp.einsum('nhc,hc->nh', h_dst, att_dst)
        e = a_src[src] + a_dst[dst]
        e = jnp.where(e > 0, e, NEG_SLOPE * e)
        m = jax.ops.segment_max(e, dst, num_segments=n)
        p = jnp.exp(e - m[dst])
        denom = jax.ops.segment_sum(p, dst, num_segments=n)
        alpha = p / jnp.maximum(denom[dst], 1e-16)
        msg = alpha[:, :, None] * h_src[src]
        out = jax.ops.segment_sum(msg, dst, num_segments=n).reshape(n, HC) + bias
        mu = out.mean(-1, keepdims=True)
        var = ((out - mu) ** 2).mean(-1, keepdims=True)
        out = (out - mu) * jax.lax.rsqrt(var + LN_EPS) * ln_gamma + ln_beta
        return jnp.where(out > 0, out, prelu_w * out)

    def _L0_ffn_ref(x, Wg, bg, bias, W1, b1, W2, b2):
        import jax, jax.numpy as jnp
        import numpy as np
        D_MODEL = 256
        EXPERT_DIM = 512
        NUM_EXPERTS = 8
        TOP_K = 2
        SEQ_LEN = 256
        BATCH = 2
        x_flat = x.reshape(-1, D_MODEL)
        gate_logits = x_flat @ Wg + bg + bias
        topk_vals, topk_idx = jax.lax.top_k(gate_logits, TOP_K)
        topk_w = jax.nn.softmax(topk_vals, axis=-1)
        combine = (jax.nn.one_hot(topk_idx, NUM_EXPERTS, dtype=x.dtype) * topk_w[..., None]).sum(axis=1)
        h = jax.nn.relu(jnp.einsum('td,edh->teh', x_flat, W1) + b1)
        y = jnp.einsum('teh,ehd->ted', h, W2) + b2
        out = jnp.einsum('ted,te->td', y, combine)
        return out.reshape(x.shape)
    edge_index = jnp.stack([src, dst])
    batch0 = jnp.zeros((6250,), jnp.int32)
    x = x + _L0_gnn_ref(_layernorm(x, axis=-1), edge_weight1, L0_gnn_W_src, L0_gnn_W_dst, L0_gnn_att_src, L0_gnn_att_dst, L0_gnn_bias, L0_gnn_ln_gamma, L0_gnn_ln_beta, L0_gnn_prelu_w, edge_index, batch0)
    x = x + _L0_ffn_ref(_layernorm(x, axis=-1)[None], L0_ffn_Wg, L0_ffn_bg, L0_ffn_bias, L0_ffn_W1, L0_ffn_b1, L0_ffn_W2, L0_ffn_b2)[0]
    return x

_drawn_inputs = setup_inputs


def setup_inputs(seed=0):
    import zlib

    import numpy as np

    out = dict(_drawn_inputs(seed))
    spreads = {'L0_gnn_bias': (0.0, 0.1),
     'L0_gnn_ln_gamma': (1.0, 0.2),
     'L0_gnn_ln_beta': (0.0, 0.1),
     'L0_gnn_prelu_w': (0.25, 0.535),
     'L0_ffn_bias': (0.0, 0.1)}
    factors = {'L0_ffn_bg': 5.13, 'L0_ffn_b1': 8.0, 'L0_ffn_b2': 4.915}
    for name, (base, spread) in spreads.items():
        noise = np.random.default_rng([zlib.crc32(name.encode()), seed]).standard_normal(out[name].shape)
        drawn = base * np.exp(spread * noise) if base else spread * noise
        out[name] = jnp.asarray(drawn.astype(out[name].dtype))
    for name, factor in factors.items():
        out[name] = (out[name] * factor).astype(out[name].dtype)
    return out
```

```python
import numpy as np
import concourse.bass as bass
from concourse import mybir
from contextlib import ExitStack

F32 = mybir.dt.float32
F32R = mybir.dt.float32r
I32 = mybir.dt.int32
ALU = mybir.AluOpType
ACT = mybir.ActivationFunctionType
AX = mybir.AxisListType

P = 128
N, D = 6250, 256
E = 100000
HEADS, HC = 4, 64
NEG_SLOPE, LN_EPS = 0.2, 1e-5
TILES = -(-N // P)
NP_ = TILES * P
PAD_NODE = NP_ - 1
CH = 7
CHUNKS = TILES // CH
ET = 8
SUP = ET * P
NSUP = -(-E // SUP)
EP = NSUP * SUP
ROW = D + HEADS
KD = D // P
NX, HID = 8, 512
KH = HID // P
GT = 4
GROUPS = TILES // GT
TINY = 1e-30

assert TILES % CH == 0 and NSUP % 2 == 0 and TILES - GROUPS * GT == 1


def hold(engine, semaphore, value, passed):
    engine.wait_ge(semaphore, value)
    engine.sem_inc(passed, 1)


def build_program(nc, x, src_idx, dst_part, dst_row, W_src, W_dst, att_src, att_dst, bias, ln_gamma, ln_beta,
                  prelu_w, Wg, bg, gbias, W1, b1, W2, b2, out):
    x_tiles = x.rearrange("(t p) d -> p t d", p=P)
    out_tiles = out.rearrange("(t p) d -> p t d", p=P)
    table = nc.dram_tensor("h_src_table", [NP_, ROW], F32).ap()
    table_tiles = table.rearrange("(t p) c -> p t c", p=P)
    bounds_dram = nc.dram_tensor("bounds_dram", [NSUP, 2], I32).ap()
    x1_dram = nc.dram_tensor("x1_dram", [NP_, D], F32).ap()
    x1_tiles = x1_dram.rearrange("(t p) d -> p t d", p=P)

    whole = ExitStack()
    with whole:
        def sb(name, shape, dt=F32, ctx=whole):
            return ctx.enter_context(nc.sbuf_tensor(name, shape, dt))

        def ps(name, shape, ctx):
            return ctx.enter_context(nc.psum_tensor(name, shape, F32))

        def sem(name):
            return whole.enter_context(nc.semaphore(name))

        ident = sb("ident", [P, P])
        eps = sb("eps", [P, 1])
        bounds = sb("bounds", [1, NSUP, 2], I32)
        bounds_in = sem("bounds_in")
        sp_passed, dve_passed, pe_passed, pool_passed = sem("sp_passed"), sem("dve_passed"), sem("pe_passed"), sem("pool_passed")

        edge_ctx = ExitStack()
        with edge_ctx:
            node_id = sb("node_id", [P, TILES], F32, edge_ctx)
            col_id = sb("col_id", [P, P], F32, edge_ctx)
            node_tab = sb("node_tab", [P, TILES, 2 * HEADS], F32, edge_ctx)

            with ExitStack() as c:
                xs = sb("xs", [P, TILES, D], F32, c)
                hs = sb("hs", [P, TILES, ROW], F32, c)
                xn = sb("xn", [P, CH, D], F32, c)
                xnT = sb("xnT", [P, CH, KD, P], F32, c)
                stats = sb("stats", [P, CH, 6], F32, c)
                meanvar = sb("meanvar", [P, CH, 2], F32, c)
                sd = sb("sd", [P, CH], F32, c)
                rstd = sb("rstd", [P, TILES], F32, c)
                nmr = sb("nmr", [P, TILES], F32, c)
                w_aug = sb("w_aug", [P, KD, D + 2 * HEADS], F32, c)
                w_dst = sb("w_dst", [P, KD, D], F32, c)
                att_b = sb("att_b", [P, 2, D], F32, c)
                prod = sb("prod", [P, KD, D], F32, c)
                gmax = sb("gmax", [P, HEADS], F32, c)
                gmax_all = sb("gmax_all", [P, HEADS], F32, c)
                shift_z = sb("shift_z", [P, TILES, HEADS], F32, c)
                rows = sb("rows", [NSUP, SUP], I32, c)
                lohi = sb("lohi", [NSUP, 2], F32, c)
                lohi_i = sb("lohi_i", [NSUP, 2], I32, c)
                node_id_i = sb("node_id_i", [P, TILES], I32, c)
                col_id_i = sb("col_id_i", [P, P], I32, c)
                ps_T = ps("ps_T", [P, 2, 512], c)
                ps_h = ps("ps_h", [P, 2, 512], c)

                x_in, w_in, rows_in, table_out = sem("x_in"), sem("w_in"), sem("rows_in"), sem("table_out")
                consts_i, consts = sem("consts_i"), sem("consts")
                stats_ready, sd_ready, rstd_ready = sem("stats_ready"), sem("sd_ready"), sem("rstd_ready")
                w_ready, xn_ready, xT_done, xT_ready = sem("w_ready"), sem("xn_ready"), sem("xT_done"), sem("xT_ready")
                h_done, h_out, gmax_ready, gmax_done = sem("h_done"), sem("h_out"), sem("gmax_ready"), sem("gmax_done")
                lohi_ready = sem("lohi_ready")

                block = c.enter_context(nc.Block())

                @block.sync
                def _(sp):
                    sp.dma_start(rows[:], dst_row).then_inc(rows_in, 16)
                    with sp.Fori(0, CHUNKS) as g:
                        sp.dma_start(xs[:, bass.ds(g * CH, CH), :], x_tiles[:, bass.ds(g * CH, CH), :]).then_inc(x_in, 16)
                        hold(sp, x_in, g * 16 + 16, sp_passed)
                    hold(sp, lohi_ready, 1, sp_passed)
                    sp.dma_start(bounds_dram, lohi_i[:]).then_inc(bounds_in, 16)
                    hold(sp, bounds_in, 16, sp_passed)
                    sp.dma_start(bounds[:], bounds_dram[None, :, :]).then_inc(bounds_in, 16)
                    hold(sp, bounds_in, 32, sp_passed)
                    with sp.Fori(0, CHUNKS) as g:
                        hold(sp, h_out, g * CH + CH + 1, sp_passed)
                        sp.dma_start(table_tiles[:, bass.ds(g * CH, CH), :], hs[:, bass.ds(g * CH, CH), :]).then_inc(table_out, 16)
                    hold(sp, table_out, 16 * CHUNKS, sp_passed)

                @block.scalar
                def _(act):
                    act.dma_start(w_aug[:, :, 0:D], W_src.rearrange("(k p) n -> p k n", p=P)).then_inc(w_in, 16)
                    act.dma_start(w_dst[:], W_dst.rearrange("(k p) n -> p k n", p=P)).then_inc(w_in, 16)
                    act.dma_start(att_b[:, 0, :], att_src.partition_broadcast(P)).then_inc(w_in, 16)
                    act.dma_start(att_b[:, 1, :], att_dst.partition_broadcast(P)).then_inc(w_in, 16)
                    act.wait_ge(consts, 1)
                    with act.Fori(0, CHUNKS) as g:
                        act.wait_ge(stats_ready, g + 1)
                        nc.scalar.activation(sd[:], meanvar[:, :, 1], ACT.Sqrt,
                                             bias=eps[:]).then_inc(sd_ready, 1)
                    with act.Fori(0, CHUNKS) as g:
                        act.wait_ge(rstd_ready, g + 1)
                        for j in range(CH):
                            t = g * CH + j
                            act.wait_ge(xT_done, t + 1)
                            nc.scalar.activation(xn[:, j, :], xs[:, bass.ds(t, 1), :], ACT.Identity,
                                                 bias=nmr[:, bass.ds(t, 1)], scale=rstd[:, bass.ds(t, 1)]).then_inc(xn_ready, 1)
                            act.wait_ge(xT_done, t + CH + 1)
                            act.wait_ge(h_done, t + 1)
                            nc.scalar.copy(xnT[:, j, :, :], ps_T[:, j % 2, 0:D]).then_inc(xT_ready, 1)

                @block.gpsimd
                def _(pool):
                    nc.gpsimd.memset(ident[:], 0.0)
                    nc.gpsimd.memset(eps[:], LN_EPS)
                    nc.gpsimd.iota(node_id_i[:], pattern=[[P, TILES]], base=0, channel_multiplier=1)
                    nc.gpsimd.iota(col_id_i[:], pattern=[[1, P]], base=0, channel_multiplier=0)
                    pool.drain()
                    nc.gpsimd.tensor_copy(node_id[:], node_id_i[:])
                    nc.gpsimd.tensor_copy(col_id[:], col_id_i[:])
                    nc.gpsimd.affine_select(out=ident[:], in_=ident[:], compare_op=ALU.not_equal, fill=1.0, base=0,
                                            pattern=[[-1, P]], channel_multiplier=1)
                    pool.drain()
                    nc.gpsimd.memset(gmax_all[:], 0.0).then_inc(consts, 1)
                    pool.wait_ge(consts, 1)
                    pool.wait_ge(gmax_ready, 1)
                    nc.gpsimd.partition_all_reduce(gmax_all[:], gmax[:], P, bass.bass_isa.ReduceOp.max).then_inc(gmax_done, 1)

                @block.vector
                def _(dve):
                    dve.sem_inc(h_out, 1)
                    dve.wait_ge(w_in, 64)
                    for side, w in ((0, w_aug[:, :, 0:D]), (1, w_dst[:])):
                        nc.vector.tensor_tensor(prod[:], w, att_b[:, side, :].unsqueeze(1).to_broadcast([P, KD, D]), ALU.mult)
                        dve.drain()
                        lo = D + side * HEADS
                        nc.vector.tensor_reduce(w_aug[:, :, lo:lo + HEADS], prod[:].rearrange("p k (h c) -> p k h c", h=HEADS),
                                                AX.X, ALU.add)
                        dve.drain()
                    nc.vector.memset(gmax[:], 0.0).then_inc(w_ready, 1)
                    dve.wait_ge(rows_in, 16)
                    nc.vector.tensor_reduce(lohi[:, 0:1], rows[:], AX.X, ALU.min)
                    nc.vector.tensor_reduce(lohi[:, 1:2], rows[:], AX.X, ALU.max)
                    dve.drain()
                    nc.vector.tensor_copy(lohi_i[:], lohi[:])
                    dve.drain()
                    nc.vector.tensor_scalar(lohi_i[:], lohi_i[:], 7, None, ALU.arith_shift_right).then_inc(lohi_ready, 1)
                    with dve.Fori(0, CHUNKS) as g:
                        dve.wait_ge(x_in, g * 16 + 16)
                        for j in range(CH):
                            nc.vector.bn_stats(stats[:, j, :], xs[:, bass.ds(g * CH + j, 1), :])
                        dve.drain()
                        for j in range(CH):
                            i = nc.vector.bn_aggr(meanvar[:, j, :], stats[:, j, :])
                        i.then_inc(stats_ready, 1)
                        dve.wait_ge(sd_ready, g + 1)
                        nc.vector.reciprocal(rstd[:, bass.ds(g * CH, CH)], sd[:])
                        dve.drain()
                        nc.vector.scalar_tensor_tensor(out=nmr[:, bass.ds(g * CH, CH)], in0=meanvar[:, :, 0],
                                                       scalar=-1.0, in1=rstd[:, bass.ds(g * CH, CH)], op0=ALU.mult,
                                                       op1=ALU.mult).then_inc(rstd_ready, 1)
                    with dve.Fori(0, CHUNKS) as g:
                        for j in range(CH):
                            t = g * CH + j
                            dve.wait_ge(h_done, t + CH + 1)
                            nc.vector.tensor_copy(hs[:, bass.ds(t, 1), :], ps_h[:, j % 2, 0:ROW])
                            nc.vector.tensor_copy(node_tab[:, bass.ds(t, 1), 0:HEADS],
                                                  ps_h[:, j % 2, ROW:ROW + HEADS]).then_inc(h_out, 1)
                    dve.drain()
                    nc.vector.tensor_reduce(gmax[:], hs[:, :, D:ROW].rearrange("p t h -> p h t"), AX.X, ALU.max).then_inc(gmax_ready, 1)
                    dve.wait_ge(gmax_done, 1)
                    nc.vector.tensor_tensor(shift_z[:], node_tab[:, :, 0:HEADS],
                                            gmax_all[:].unsqueeze(1).to_broadcast([P, TILES, HEADS]), ALU.add)
                    dve.drain()
                    nc.vector.scalar_tensor_tensor(out=node_tab[:, :, HEADS:2 * HEADS], in0=shift_z[:], scalar=NEG_SLOPE,
                                                   in1=shift_z[:], op0=ALU.mult, op1=ALU.max)

                @block.tensor
                def _(pe):
                    pe.sem_inc(xT_done, CH)
                    pe.sem_inc(h_done, CH)
                    pe.wait_ge(consts, 1)
                    pe.wait_ge(w_ready, 1)
                    with pe.Fori(0, CHUNKS) as g:
                        for j in range(CH):
                            t = g * CH + j
                            pe.wait_ge(xn_ready, t + 1)
                            for k in range(KD):
                                i = nc.tensor.transpose(ps_T[:, j % 2, k * P:(k + 1) * P], xn[:, j, k * P:(k + 1) * P], ident[:])
                            i.then_inc(xT_done, 1)
                            pe.wait_ge(xT_ready, t + 1)
                            pe.wait_ge(h_out, t + 1 if j == 0 else t)
                            for k in range(KD):
                                i = nc.tensor.matmul(ps_h[:, j % 2, 0:D + 2 * HEADS], xnT[:, j, k, :], w_aug[:, k, :],
                                                     start=(k == 0), stop=(k == KD - 1))
                            i.then_inc(h_done, 1)

            mid_ctx = ExitStack()
            with mid_ctx:
                acc = sb("acc", [P, TILES + 1, ROW], F32, mid_ctx)
                with ExitStack() as edge2:
                    edge_tab = sb("edge_tab", [P, NSUP + 1, ET, 2 * HEADS], F32, edge2)

                    with ExitStack() as c:
                        row_b = sb("row_b", [P, 2, SUP], I32, c)
                        sel = sb("sel", [P, 2, SUP // 2], F32, c)
                        ps_te = ps("ps_te", [P, ET, 2 * HEADS], c)
                        row_in = [sem(f"row_in{u}") for u in range(2)]
                        row_used = sem("row_used")
                        sel_ready = [sem(f"sel_ready{h}") for h in range(2)]
                        te_done = [sem(f"te_done{h}") for h in range(2)]
                        te_out, te_zero = sem("te_out"), sem("te_zero")
                        block = c.enter_context(nc.Block())

                        @block.sync
                        def _(sp):
                            with sp.Fori(0, NSUP // 2) as i:
                                for u in range(2):
                                    hold(sp, row_used, 2 * i + u + 1, sp_passed)
                                    sp.dma_start(row_b[:, u, :], dst_row[bass.ds(2 * i + u, 1), :].partition_broadcast(P)
                                                 ).then_inc(row_in[u], 16)

                        @block.gpsimd
                        def _(pool):
                            nc.gpsimd.memset(acc[:], 0.0)

                        @block.vector
                        def _(dve):
                            dve.sem_inc(row_used, 2)
                            nc.vector.memset(edge_tab[:], 0.0)
                            nc.vector.memset(ps_te[:], 0.0)
                            dve.drain()
                            pair, s_prev = dve.alloc_register("pair2"), dve.alloc_register("s_prev2")
                            dve.reg_mov(pair, 1)
                            dve.reg_mov(s_prev, NSUP)

                            def add_last():
                                s = dve.snap(s_prev, min_val=0, max_val=NSUP)
                                nc.vector.tensor_tensor(edge_tab[:, bass.ds(s, 1), :, :], edge_tab[:, bass.ds(s, 1), :, :],
                                                        ps_te[:].unsqueeze(1), ALU.add).then_inc(te_out, 1)

                            with dve.Fori(0, NSUP // 2) as i:
                                for u in range(2):
                                    s = 2 * i + u
                                    lo = dve.value_load(bounds[0:1, bass.ds(s, 1), 0], min_val=0, max_val=TILES - 1)
                                    hi = dve.value_load(bounds[0:1, bass.ds(s, 1), 1], min_val=0, max_val=TILES - 1)
                                    hold(dve, row_in[u], 16 * i + 16, dve_passed)
                                    with dve.Fori(lo, hi + 1) as b:
                                        n = dve.snap(pair)
                                        for h in range(2):
                                            dve.wait_ge(te_done[h], n)
                                            if h == 1:
                                                add_last()
                                            nc.vector.tensor_scalar(sel[:, h, :], row_b[:, u, h * (SUP // 2):(h + 1) * (SUP // 2)],
                                                                    node_id[:, bass.ds(b, 1)], None, ALU.is_equal
                                                                    ).then_inc(sel_ready[h], 1)
                                        dve.reg_add(pair, pair, 1)
                                        dve.reg_mov(s_prev, s)
                                    dve.drain().then_inc(row_used, 1)
                            n = dve.snap(pair)
                            dve.wait_ge(te_done[1], n)
                            add_last()

                        @block.tensor
                        def _(pe):
                            pe.sem_inc(te_done[0], 1)
                            pe.sem_inc(te_done[1], 1)
                            pair = pe.alloc_register("pair2")
                            pe.reg_mov(pair, 1)
                            with pe.Fori(0, NSUP) as s:
                                lo = pe.value_load(bounds[0:1, bass.ds(s, 1), 0], min_val=0, max_val=TILES - 1)
                                hi = pe.value_load(bounds[0:1, bass.ds(s, 1), 1], min_val=0, max_val=TILES - 1)
                                with pe.Fori(lo, hi + 1) as b:
                                    n = pe.snap(pair)
                                    for h in range(2):
                                        pe.wait_ge(sel_ready[h], n)
                                        if h == 0:
                                            pe.wait_ge(te_out, n)
                                        for r in range(ET // 2):
                                            m = nc.tensor.matmul(ps_te[:, h * (ET // 2) + r, :], sel[:, h, r * P:(r + 1) * P],
                                                                 node_tab[:, bass.ds(b, 1), :], start=True, stop=True)
                                        m.then_inc(te_done[h], 1)
                                    pe.reg_add(pair, pair, 1)

                    with ExitStack() as c:
                        msg = sb("msg", [P, 2, ET, ROW], F32, c)
                        idx = sb("idx", [P, 2, ET], I32, c)
                        dst_i = sb("dst_i", [P, NSUP * ET], I32, c)
                        dst_f = sb("dst_f", [P, NSUP * ET], F32, c)
                        block_base = sb("block_base", [P, TILES], F32, c)
                        sel = sb("sel3", [P, 2, ET // 2, P], F32, c)
                        score = sb("score", [P, 2, ET, HEADS], F32, c)
                        ps_agg = ps("ps_agg", [P, 512], c)
                        idx_in = [sem(f"idx_in{u}") for u in range(2)]
                        gathered = [sem(f"gathered{u}") for u in range(2)]
                        dst_in, score_ready, p_ready, msg_ready = sem("dst_in"), sem("score_ready"), sem("p_ready"), sem("msg_ready")
                        msg_used = sem("msg_used")
                        sel_ready = [sem(f"sel3_ready{h}") for h in range(2)]
                        agg_done = [sem(f"agg_done{h}") for h in range(2)]
                        added = sem("added")
                        block = c.enter_context(nc.Block())

                        @block.sync
                        def _(sp):
                            for u in range(2):
                                sp.dma_start(idx[:, u, :], src_idx[u]).then_inc(idx_in[u], 16)
                            sp.dma_start(dst_i[:], dst_part).then_inc(dst_in, 16)
                            with sp.Fori(0, NSUP // 2 - 1) as i:
                                for u in range(2):
                                    hold(sp, gathered[u], (16 * ET) * i + 16 * ET, sp_passed)
                                    sp.dma_start(idx[:, u, :], src_idx[bass.ds(2 * i + 2 + u, 1)].rearrange("a p r -> (a p) r")
                                                 ).then_inc(idx_in[u], 16)

                        @block.gpsimd
                        def _(pool):
                            with pool.Fori(0, NSUP // 2) as i:
                                for u in range(2):
                                    pool.wait_ge(idx_in[u], 16 * i + 16)
                                    hold(pool, msg_used, 2 * i + u + 1, pool_passed)
                                    for r in range(ET):
                                        nc.gpsimd.indirect_dma_start(
                                            out=msg[:, u, r, :], out_offset=None, in_=table,
                                            in_offset=bass.IndirectOffsetOnAxis(ap=idx[:, u, r:r + 1], axis=0)
                                        ).then_inc(gathered[u], 16)

                        @block.scalar
                        def _(act):
                            with act.Fori(0, NSUP // 2) as i:
                                for u in range(2):
                                    act.wait_ge(score_ready, 2 * i + u + 1)
                                    nc.scalar.activation(msg[:, u, :, D:ROW], score[:, u, :, :], ACT.Exp).then_inc(p_ready, 1)

                        @block.vector
                        def _(dve):
                            dve.wait_ge(dst_in, 16)
                            nc.vector.tensor_copy(dst_f[:], dst_i[:])
                            nc.vector.tensor_scalar(block_base[:], node_id[:], node_id[:, 0:1], None, ALU.subtract)
                            nc.vector.memset(ps_agg[:], 0.0)
                            dve.drain()
                            pair, b_prev = dve.alloc_register("pair3"), dve.alloc_register("b_prev3")
                            dve.reg_mov(pair, 1)
                            dve.reg_mov(b_prev, TILES)

                            def add_last():
                                b = dve.snap(b_prev, min_val=0, max_val=TILES)
                                nc.vector.tensor_tensor(acc[:, bass.ds(b, 1), :], acc[:, bass.ds(b, 1), :],
                                                        ps_agg[:, 0:ROW].unsqueeze(1), ALU.add).then_inc(added, 1)

                            with dve.Fori(0, NSUP // 2) as i:
                                for u in range(2):
                                    s = 2 * i + u
                                    lo = dve.value_load(bounds[0:1, bass.ds(s, 1), 0], min_val=0, max_val=TILES - 1)
                                    hi = dve.value_load(bounds[0:1, bass.ds(s, 1), 1], min_val=0, max_val=TILES - 1)
                                    dve.wait_ge(gathered[u], (16 * ET) * i + 16 * ET)
                                    sc = score[:, u, :, :]
                                    tab = edge_tab[:, bass.ds(s, 1), :, :].rearrange("p a r c -> p (a r) c")
                                    nc.vector.tensor_tensor(sc, msg[:, u, :, D:ROW], tab[:, :, 0:HEADS], ALU.add)
                                    dve.drain()
                                    nc.vector.scalar_tensor_tensor(out=sc, in0=sc, scalar=NEG_SLOPE, in1=sc, op0=ALU.mult, op1=ALU.max)
                                    dve.drain()
                                    nc.vector.tensor_tensor(sc, sc, tab[:, :, HEADS:2 * HEADS], ALU.subtract).then_inc(score_ready, 1)
                                    dve.wait_ge(p_ready, s + 1)
                                    h4 = msg[:, u, :, 0:D].rearrange("p r (h c) -> p r h c", h=HEADS)
                                    nc.vector.tensor_tensor(h4, h4, msg[:, u, :, D:ROW].unsqueeze(3).to_broadcast([P, ET, HEADS, HC]),
                                                            ALU.mult).then_inc(msg_ready, 1)
                                    with dve.Fori(lo, hi + 1) as b:
                                        n = dve.snap(pair)
                                        for h in range(2):
                                            dve.wait_ge(agg_done[h], n)
                                            if h == 1:
                                                add_last()
                                            dst = dst_f[:, bass.ds(s * ET + h * (ET // 2), ET // 2)]
                                            nc.vector.scalar_tensor_tensor(
                                                out=sel[:, h, :, :], in0=col_id[:].unsqueeze(1).to_broadcast([P, ET // 2, P]),
                                                scalar=block_base[:, bass.ds(b, 1)], in1=dst.unsqueeze(2).to_broadcast([P, ET // 2, P]),
                                                op0=ALU.add, op1=ALU.is_equal).then_inc(sel_ready[h], 1)
                                        dve.reg_add(pair, pair, 1)
                                        dve.reg_mov(b_prev, b)
                            n = dve.snap(pair)
                            dve.wait_ge(agg_done[1], n)
                            add_last()

                        @block.tensor
                        def _(pe):
                            pe.sem_inc(agg_done[0], 1)
                            pe.sem_inc(agg_done[1], 1)
                            pe.sem_inc(msg_used, 2)
                            pair = pe.alloc_register("pair3")
                            pe.reg_mov(pair, 1)
                            with pe.Fori(0, NSUP // 2) as i:
                                for u in range(2):
                                    s = 2 * i + u
                                    lo = pe.value_load(bounds[0:1, bass.ds(s, 1), 0], min_val=0, max_val=TILES - 1)
                                    hi = pe.value_load(bounds[0:1, bass.ds(s, 1), 1], min_val=0, max_val=TILES - 1)
                                    hold(pe, msg_ready, s + 1, pe_passed)
                                    with pe.Fori(lo, hi + 1) as b:
                                        n = pe.snap(pair)
                                        for h in range(2):
                                            pe.wait_ge(sel_ready[h], n)
                                            if h == 0:
                                                pe.wait_ge(added, n)
                                            for r in range(h * (ET // 2), (h + 1) * (ET // 2)):
                                                m = nc.tensor.matmul(ps_agg[:, 0:ROW], sel[:, h, r % (ET // 2), :], msg[:, u, r, :],
                                                                     start=(r == 0), stop=(r == ET - 1))
                                            m.then_inc(agg_done[h], 1)
                                        pe.reg_add(pair, pair, 1)
                                    pe.drain().then_inc(msg_used, 1)

                with ExitStack() as c:
                    xr = sb("xr", [P, CH, D], F32, c)
                    o = sb("o", [P, CH, D], F32, c)
                    pos = sb("pos", [P, CH, D], F32, c)
                    x1 = sb("x1", [P, CH, D], F32, c)
                    rden = sb("rden", [P, TILES, HEADS], F32, c)
                    vec = sb("vec", [P, 4, D], F32, c)
                    stats = sb("stats4", [P, CH, 6], F32, c)
                    meanvar = sb("meanvar4", [P, CH, 2], F32, c)
                    sd = sb("sd4", [P, CH], F32, c)
                    rstd = sb("rstd4", [P, CH], F32, c)
                    nmr = sb("nmr4", [P, CH], F32, c)
                    vec_in, xr_in, x1_stored = sem("vec_in"), sem("xr_in"), sem("x1_stored")
                    stats_ready, sd_ready, rstd_ready = sem("stats4_ready"), sem("sd4_ready"), sem("rstd4_ready")
                    norm_ready, y_ready, pos_ready, x1_ready, x_added = sem("norm4_ready"), sem("y4_ready"), sem("pos4_ready"), sem("x1_ready"), sem("x4_added")
                    block = c.enter_context(nc.Block())

                    def row(k):
                        return vec[:, k, :].unsqueeze(1).to_broadcast([P, CH, D])

                    @block.sync
                    def _(sp):
                        for k, v in enumerate((bias, ln_gamma, ln_beta, prelu_w)):
                            sp.dma_start(vec[:, k, :], v.partition_broadcast(P)).then_inc(vec_in, 16)
                        with sp.Fori(0, CHUNKS) as g:
                            hold(sp, x1_ready, g + 1, sp_passed)
                            sp.dma_start(xr[:], x_tiles[:, bass.ds(g * CH, CH), :]).then_inc(xr_in, 16)
                            hold(sp, x1_ready, g + 2, sp_passed)
                            sp.dma_start(x1_tiles[:, bass.ds(g * CH, CH), :], x1[:]).then_inc(x1_stored, 16)
                            hold(sp, x1_stored, 16 * g + 32, sp_passed)

                    @block.gpsimd
                    def _(pool):
                        with pool.Fori(0, CHUNKS) as g:
                            pool.wait_ge(xr_in, 16 * g + 16)
                            pool.wait_ge(pos_ready, g + 1)
                            nc.gpsimd.tensor_tensor(xr[:], xr[:], pos[:], ALU.add).then_inc(x_added, 1)

                    @block.scalar
                    def _(act):
                        with act.Fori(0, CHUNKS) as g:
                            act.wait_ge(stats_ready, g + 1)
                            nc.scalar.activation(sd[:], meanvar[:, :, 1], ACT.Sqrt, bias=eps[:]).then_inc(sd_ready, 1)
                            act.wait_ge(rstd_ready, g + 1)
                            for j in range(CH):
                                i = nc.scalar.activation(o[:, j, :], o[:, j, :], ACT.Identity, bias=nmr[:, j:j + 1], scale=rstd[:, j:j + 1])
                            i.then_inc(norm_ready, 1)
                            act.wait_ge(y_ready, g + 1)
                            nc.scalar.activation(pos[:], o[:], ACT.Relu).then_inc(pos_ready, 1)

                    @block.vector
                    def _(dve):
                        dve.sem_inc(x1_ready, 1)
                        dve.sem_inc(x1_stored, 16)
                        nc.vector.tensor_scalar(rden[:], acc[:, 0:TILES, D:ROW], TINY, None, ALU.max)
                        dve.drain()
                        nc.vector.reciprocal(rden[:], rden[:])
                        dve.drain()
                        dve.wait_ge(vec_in, 64)
                        with dve.Fori(0, CHUNKS) as g:
                            dve.drain()
                            nc.vector.tensor_tensor(o[:].rearrange("p t (h c) -> p t h c", h=HEADS),
                                                    acc[:, bass.ds(g * CH, CH), 0:D].rearrange("p t (h c) -> p t h c", h=HEADS),
                                                    rden[:, bass.ds(g * CH, CH), :].unsqueeze(3).to_broadcast([P, CH, HEADS, HC]), ALU.mult)
                            dve.drain()
                            nc.vector.tensor_tensor(o[:], o[:], row(0), ALU.add)
                            dve.drain()
                            for j in range(CH):
                                nc.vector.bn_stats(stats[:, j, :], o[:, j, :])
                            dve.drain()
                            for j in range(CH):
                                i = nc.vector.bn_aggr(meanvar[:, j, :], stats[:, j, :])
                            i.then_inc(stats_ready, 1)
                            dve.wait_ge(sd_ready, g + 1)
                            nc.vector.reciprocal(rstd[:], sd[:])
                            dve.drain()
                            nc.vector.scalar_tensor_tensor(out=nmr[:], in0=meanvar[:, :, 0], scalar=-1.0, in1=rstd[:],
                                                           op0=ALU.mult, op1=ALU.mult).then_inc(rstd_ready, 1)
                            dve.wait_ge(norm_ready, g + 1)
                            nc.vector.tensor_tensor(o[:], o[:], row(1), ALU.mult)
                            dve.drain()
                            nc.vector.tensor_tensor(o[:], o[:], row(2), ALU.add).then_inc(y_ready, 1)
                            dve.wait_ge(pos_ready, g + 1)
                            nc.vector.scalar_tensor_tensor(out=o[:], in0=o[:], scalar=0.0, in1=row(3), op0=ALU.min, op1=ALU.mult)
                            dve.drain()
                            dve.wait_ge(x_added, g + 1)
                            dve.wait_ge(x1_stored, 16 * g + 16)
                            nc.vector.tensor_tensor(x1[:], xr[:], o[:], ALU.add).then_inc(x1_ready, 1)

        with ExitStack() as c:
            w1h = sb("w1h", [P, NX, KD, HID], F32R, c)
            w1l = sb("w1l", [P, NX, KD, HID], F32R, c)
            w2h = sb("w2h", [P, NX, KH, D], F32R, c)
            w2l = sb("w2l", [P, NX, KH, D], F32R, c)
            raw = sb("raw", [P, 2, KD * HID], F32, c)
            wgh = sb("wgh", [P, KD, NX], F32R, c)
            wgl = sb("wgl", [P, KD, NX], F32R, c)
            wg = sb("wg", [P, KD, NX], F32, c)
            gate_b = sb("gate_b", [P, 2, NX], F32, c)
            b1_rows = sb("b1_rows", [NX * KH, P], F32, c)
            b1T = sb("b1T", [P, NX * KH], F32, c)
            b2_sb = sb("b2_sb", [NX, D], F32, c)
            ramp_i = sb("ramp_i", [P, GT, NX], I32, c)
            ramp = sb("ramp", [P, GT, NX], F32, c)
            y = sb("y", [P, 2 * GT, D], F32, c)
            xn = sb("xn5", [P, GT, D], F32, c)
            xTh = sb("xTh", [P, KD, GT * P], F32R, c)
            xTl = sb("xTl", [P, KD, GT * P], F32R, c)
            h32 = sb("h32", [P, KH, GT * P], F32, c)
            hh = sb("hh", [P, KH, GT * P], F32R, c)
            hl = sb("hl", [P, KH, GT * P], F32R, c)
            stats = sb("stats5", [P, GT, 6], F32, c)
            meanvar = sb("meanvar5", [P, GT, 2], F32, c)
            sd = sb("sd5", [P, GT], F32, c)
            rstd = sb("rstd5", [P, GT], F32, c)
            nmr = sb("nmr5", [P, GT], F32, c)
            logit = sb("logit", [P, GT, NX], F32, c)
            work = sb("work", [P, GT, NX], F32, c)
            pick = sb("pick", [P, 2, GT, NX], F32, c)
            top = sb("top", [P, 2, GT], F32, c)
            first = sb("first", [P, GT], F32, c)
            gap = sb("gap", [P, GT], F32, c)
            wts = sb("wts", [P, 2, GT], F32, c)
            comb = sb("comb", [P, GT, NX], F32, c)
            combT = sb("combT", [NX, GT, P], F32, c)
            ps_h = ps("ps_h5", [P, KH, 512], c)
            ps_y = ps("ps_y5", [P, GT, 512], c)

            small_in, raw_in, raw_used = sem("small_in"), [sem("raw_in0"), sem("raw_in1")], sem("raw_used")
            ramp_ready, b1T_done, b1T_ready, weights_ready = sem("ramp_ready"), sem("b1T_done"), sem("b1T_ready"), sem("weights_ready")
            x1_in, y_out = sem("x1_in"), sem("y_out")
            stats_ready, sd_ready, rstd_ready = sem("stats5_ready"), sem("sd5_ready"), sem("rstd5_ready")
            xn_ready, xT_done, xh_ready, xl_ready = sem("xn5_ready"), sem("xT5_done"), sem("xh_ready"), sem("xl_ready")
            logit_done, gap_ready, e_ready = sem("logit_done"), sem("gap_ready"), sem("e_ready")
            comb_ready, combT_done, combT_ready, b2_done, b2_added = (sem("comb_ready"), sem("combT_done"), sem("combT_ready"),
                                                                      sem("b2_done"), sem("b2_added"))
            h_done, h_out, hT_ready, w2_done, y_done, y_added = (sem("h5_done"), sem("h5_out"), sem("hT_ready"), sem("w2_done"),
                                                                 sem("y5_done"), sem("y5_added"))
            HU = NX * KH
            block = c.enter_context(nc.Block())

            def groups(engine, body):
                with engine.Fori(0, GROUPS) as g:
                    body(g, g * GT, GT, (g % 2) * GT, g * (NX * GT))
                body(GROUPS, GROUPS * GT, 1, (GROUPS % 2) * GT, GROUPS * NX * GT)

            @block.sync
            def _(sp):
                sp.dma_start(wg[:], Wg.rearrange("(k p) n -> p k n", p=P)).then_inc(small_in, 16)
                sp.dma_start(gate_b[:, 0, :], bg.partition_broadcast(P)).then_inc(small_in, 16)
                sp.dma_start(gate_b[:, 1, :], gbias.partition_broadcast(P)).then_inc(small_in, 16)
                sp.dma_start(b1_rows[:], b1.rearrange("e (k p) -> (e k) p", p=P)).then_inc(small_in, 16)
                sp.dma_start(b2_sb[:], b2).then_inc(small_in, 16)
                for g in range(2):
                    sp.dma_start(y[:, g * GT:(g + 1) * GT, :], x1_tiles[:, g * GT:(g + 1) * GT, :]).then_inc(x1_in, 16)
                    hold(sp, x1_in, 16 * g + 16, sp_passed)
                with sp.Fori(0, NX) as e:
                    hold(sp, raw_used, 2 * e + 1, sp_passed)
                    sp.dma_start(raw[:, 0, :].rearrange("p (k n) -> p k n", k=KD),
                                 W1[bass.ds(e, 1)].rearrange("a (k p) n -> p (a k) n", p=P)).then_inc(raw_in[0], 16)
                    hold(sp, raw_used, 2 * e + 2, sp_passed)
                    sp.dma_start(raw[:, 1, :].rearrange("p (k n) -> p k n", k=KH),
                                 W2[bass.ds(e, 1)].rearrange("a (k p) n -> p (a k) n", p=P)).then_inc(raw_in[1], 16)

                def store(g, slot, tile, tiles):
                    sp.dma_start(out_tiles[:, bass.ds(tile, tiles), :] if not isinstance(tile, int) else out_tiles[:, tile:tile + tiles, :],
                                 y[:, bass.ds(slot, tiles), :] if not isinstance(slot, int) else y[:, slot:slot + tiles, :]
                                 ).then_inc(y_out, 16)
                    hold(sp, y_out, 16 * g + 16, sp_passed)

                with sp.Fori(0, GROUPS - 2) as g:
                    hold(sp, y_added, g * (NX * GT) + NX * GT, sp_passed)
                    store(g, (g % 2) * GT, g * GT, GT)
                    sp.dma_start(y[:, bass.ds((g % 2) * GT, GT), :], x1_tiles[:, bass.ds(g * GT + 2 * GT, GT), :]).then_inc(x1_in, 16)
                for g in (GROUPS - 2, GROUPS - 1):
                    hold(sp, y_added, (g + 1) * NX * GT, sp_passed)
                    store(g, (g % 2) * GT, g * GT, GT)
                    if g == GROUPS - 2:
                        slot = (GROUPS % 2) * GT
                        sp.dma_start(y[:, slot:slot + 1, :], x1_tiles[:, GROUPS * GT:TILES, :]).then_inc(x1_in, 16)
                hold(sp, y_added, GROUPS * NX * GT + NX, sp_passed)
                store(GROUPS, (GROUPS % 2) * GT, GROUPS * GT, 1)

            @block.gpsimd
            def _(pool):
                nc.gpsimd.iota(ramp_i[:], pattern=[[0, GT], [1, NX]], base=-NX, channel_multiplier=0)
                pool.drain()
                nc.gpsimd.tensor_copy(ramp[:], ramp_i[:]).then_inc(ramp_ready, 1)

            @block.scalar
            def _(act):
                act.wait_ge(b1T_done, 1)
                nc.scalar.copy(b1T[:], ps_y[:, 0, 0:NX * KH]).then_inc(b1T_ready, 1)

                def body(g, tile, tiles, slot, ybase):
                    cols = tiles * P
                    act.wait_ge(stats_ready, g + 1)
                    nc.scalar.activation(sd[:, 0:tiles], meanvar[:, 0:tiles, 1], ACT.Sqrt, bias=eps[:]).then_inc(sd_ready, 1)
                    act.wait_ge(rstd_ready, g + 1)
                    for j in range(tiles):
                        i = nc.scalar.activation(xn[:, j, :], y[:, bass.ds(slot + j, 1), :] if not isinstance(slot, int) else y[:, slot + j, :],
                                                 ACT.Identity, bias=nmr[:, j:j + 1], scale=rstd[:, j:j + 1])
                    i.then_inc(xn_ready, 1)
                    act.wait_ge(xT_done, g + 1)
                    for k in range(KD):
                        nc.scalar.copy(xTh[:, k, 0:cols], ps_h[:, k, 0:cols]).then_inc(xh_ready, 1)
                    act.wait_ge(gap_ready, g + 1)
                    nc.scalar.activation(wts[:, 1, 0:tiles], gap[:, 0:tiles], ACT.Exp).then_inc(e_ready, 1)
                    act.wait_ge(combT_done, g + 1)
                    nc.scalar.copy(combT[:, 0:tiles, :], ps_h[0:NX, 3, 0:cols]).then_inc(combT_ready, 1)
                    for n in range(HU):
                        act.wait_ge(h_done, g * HU + n + 1)
                        act.wait_ge(hT_ready, g * HU + n + 1)
                        nc.scalar.activation(h32[:, n % KH, 0:cols], ps_h[:, n % KH, 0:cols], ACT.Relu,
                                             bias=b1T[:, n:n + 1]).then_inc(h_out, 1)

                groups(act, body)

            @block.vector
            def _(dve):
                dve.sem_inc(hT_ready, KH)
                dve.sem_inc(raw_used, 2)
                dve.wait_ge(small_in, 80)
                nc.vector.tensor_copy(wgh[:], wg[:])
                nc.vector.tensor_tensor(gate_b[:, 0, :], gate_b[:, 0, :], gate_b[:, 1, :], ALU.add)
                dve.drain()
                nc.vector.tensor_tensor(wgl[:], wg[:], wgh[:].bitcast(F32), ALU.subtract)
                with dve.Fori(0, NX) as e:
                    for u, (hi, lo) in enumerate(((w1h, w1l), (w2h, w2l))):
                        hi_e = hi[:, bass.ds(e, 1)].rearrange("p a k n -> p (a k n)")
                        lo_e = lo[:, bass.ds(e, 1)].rearrange("p a k n -> p (a k n)")
                        dve.wait_ge(raw_in[u], 16 * e + 16)
                        nc.vector.tensor_copy(hi_e, raw[:, u, :])
                        dve.drain()
                        nc.vector.tensor_tensor(lo_e, raw[:, u, :], hi_e.bitcast(F32), ALU.subtract).then_inc(raw_used, 1)
                dve.drain().then_inc(weights_ready, 1)

                def body(g, tile, tiles, slot, ybase):
                    cols = tiles * P

                    def yt(j):
                        return y[:, slot + j, :] if isinstance(slot, int) else y[:, bass.ds(slot + j, 1), :].rearrange("p a d -> p (a d)")

                    dve.wait_ge(x1_in, 16 * g + 16)
                    for j in range(tiles):
                        nc.vector.bn_stats(stats[:, j, :], yt(j))
                    dve.drain()
                    for j in range(tiles):
                        i = nc.vector.bn_aggr(meanvar[:, j, :], stats[:, j, :])
                    i.then_inc(stats_ready, 1)
                    dve.wait_ge(sd_ready, g + 1)
                    nc.vector.reciprocal(rstd[:, 0:tiles], sd[:, 0:tiles])
                    dve.drain()
                    nc.vector.scalar_tensor_tensor(out=nmr[:, 0:tiles], in0=meanvar[:, 0:tiles, 0], scalar=-1.0, in1=rstd[:, 0:tiles],
                                                   op0=ALU.mult, op1=ALU.mult).then_inc(rstd_ready, 1)
                    for k in range(KD):
                        dve.wait_ge(xh_ready, g * KD + k + 1)
                        nc.vector.tensor_tensor(xTl[:, k, 0:cols], ps_h[:, k, 0:cols], xTh[:, k, 0:cols].bitcast(F32),
                                                ALU.subtract).then_inc(xl_ready, 1)
                    dve.wait_ge(logit_done, g + 1)
                    dve.wait_ge(ramp_ready, 1)
                    lg, wk, rp = logit[:, 0:tiles, :], work[:, 0:tiles, :], ramp[:, 0:tiles, :]

                    def wide(v):
                        return v.unsqueeze(2).to_broadcast([P, tiles, NX])

                    nc.vector.tensor_tensor(lg, ps_h[:, 2, 0:tiles * NX].rearrange("p (t e) -> p t e", e=NX),
                                            gate_b[:, 0, :].unsqueeze(1).to_broadcast([P, tiles, NX]), ALU.add)
                    dve.drain()
                    for q in range(2):
                        nc.vector.tensor_reduce(top[:, q, 0:tiles], lg, AX.X, ALU.max)
                        dve.drain()
                        nc.vector.tensor_tensor(wk, lg, wide(top[:, q, 0:tiles]), ALU.is_equal)
                        dve.drain()
                        nc.vector.tensor_tensor(wk, wk, rp, ALU.mult)
                        dve.drain()
                        nc.vector.tensor_reduce(first[:, 0:tiles], wk, AX.X, ALU.min)
                        dve.drain()
                        nc.vector.tensor_tensor(pick[:, q, 0:tiles, :], rp, wide(first[:, 0:tiles]), ALU.is_equal)
                        dve.drain()
                        if q == 0:
                            nc.vector.tensor_scalar(wk, pick[:, 0, 0:tiles, :], -3e38, None, ALU.mult)
                            dve.drain()
                            nc.vector.tensor_tensor(lg, lg, wk, ALU.add)
                            dve.drain()
                    nc.vector.tensor_tensor(gap[:, 0:tiles], top[:, 1, 0:tiles], top[:, 0, 0:tiles], ALU.subtract).then_inc(gap_ready, 1)
                    dve.wait_ge(e_ready, g + 1)
                    nc.vector.tensor_scalar(wts[:, 0, 0:tiles], wts[:, 1, 0:tiles], 1.0, None, ALU.add)
                    dve.drain()
                    nc.vector.reciprocal(wts[:, 0, 0:tiles], wts[:, 0, 0:tiles])
                    dve.drain()
                    nc.vector.tensor_tensor(wts[:, 1, 0:tiles], wts[:, 1, 0:tiles], wts[:, 0, 0:tiles], ALU.mult)
                    dve.drain()
                    for q in range(2):
                        pk = pick[:, q, 0:tiles, :]
                        nc.vector.tensor_tensor(pk, pk, wide(wts[:, q, 0:tiles]), ALU.mult)
                    dve.drain()
                    nc.vector.tensor_tensor(comb[:, 0:tiles, :], pick[:, 0, 0:tiles, :], pick[:, 1, 0:tiles, :], ALU.add).then_inc(comb_ready, 1)
                    for j in range(tiles):
                        if j == 0:
                            dve.wait_ge(b2_done, g + 1)
                        i = nc.vector.tensor_tensor(yt(j), yt(j), ps_y[:, j, 0:D], ALU.add)
                    i.then_inc(b2_added, 1)
                    dve.drain()

                    def split(e):
                        for k in range(KH):
                            n = e * KH + k
                            dve.wait_ge(h_out, g * HU + n + 1)
                            if k < KH - 1:
                                dve.wait_ge(w2_done, g * (NX * (KH - 1)) + e * (KH - 1) + k + 1)
                            else:
                                dve.wait_ge(y_done, ybase + e * tiles + 1)
                            nc.vector.tensor_copy(hh[:, k, 0:cols], h32[:, k, 0:cols])
                            dve.drain()
                            nc.vector.tensor_tensor(hl[:, k, 0:cols], h32[:, k, 0:cols], hh[:, k, 0:cols].bitcast(F32),
                                                    ALU.subtract).then_inc(hT_ready, 1)

                    split(0)
                    for e in range(NX):
                        if e + 1 < NX:
                            split(e + 1)
                        for j in range(tiles):
                            dve.wait_ge(y_done, ybase + e * tiles + j + 2)
                            nc.vector.scalar_tensor_tensor(out=yt(j), in0=ps_y[:, j, 0:D], scalar=comb[:, j, e:e + 1], in1=yt(j),
                                                           op0=ALU.mult, op1=ALU.add).then_inc(y_added, 1)

                groups(dve, body)

            @block.tensor
            def _(pe):
                pe.sem_inc(w2_done, KH - 1)
                pe.sem_inc(y_done, 1)
                pe.wait_ge(small_in, 80)
                nc.tensor.transpose(ps_y[:, 0, 0:NX * KH], b1_rows[:], ident[0:NX * KH, 0:NX * KH]).then_inc(b1T_done, 1)
                pe.wait_ge(b1T_ready, 1)
                pe.wait_ge(weights_ready, 1)

                def three(out_, ah, al, bh, bl, start, stop):
                    nc.tensor.matmul(out_, ah, bh, start=start, stop=False)
                    nc.tensor.matmul(out_, ah, bl, start=False, stop=False)
                    return nc.tensor.matmul(out_, al, bh, start=False, stop=stop)

                def body(g, tile, tiles, slot, ybase):
                    cols = tiles * P
                    pe.wait_ge(xn_ready, g + 1)
                    for k in range(KD):
                        for j in range(tiles):
                            i = nc.tensor.transpose(ps_h[:, k, j * P:(j + 1) * P], xn[:, j, k * P:(k + 1) * P], ident[:])
                    i.then_inc(xT_done, 1)
                    pe.wait_ge(xh_ready, g * KD + KD)
                    pe.wait_ge(xl_ready, g * KD + KD)
                    for j in range(tiles):
                        for k in range(KD):
                            i = three(ps_h[:, 2, j * NX:(j + 1) * NX], xTh[:, k, j * P:(j + 1) * P], xTl[:, k, j * P:(j + 1) * P],
                                      wgh[:, k, :], wgl[:, k, :], k == 0, k == KD - 1)
                    i.then_inc(logit_done, 1)
                    pe.wait_ge(comb_ready, g + 1)
                    for j in range(tiles):
                        i = nc.tensor.transpose(ps_h[0:NX, 3, j * P:(j + 1) * P], comb[:, j, :], ident[:])
                    i.then_inc(combT_done, 1)
                    pe.wait_ge(combT_ready, g + 1)
                    for j in range(tiles):
                        i = nc.tensor.matmul(ps_y[:, j, 0:D], combT[:, j, :], b2_sb[:], start=True, stop=True)
                    i.then_inc(b2_done, 1)

                    def first_layer(e):
                        for m in range(KH):
                            n = e * KH + m
                            if e > 0:
                                pe.wait_ge(h_out, g * HU + n - KH + 1)
                            for k in range(KD):
                                i = three(ps_h[:, m, 0:cols], w1h[:, e, k, m * P:(m + 1) * P], w1l[:, e, k, m * P:(m + 1) * P],
                                          xTh[:, k, 0:cols], xTl[:, k, 0:cols], k == 0, k == KD - 1)
                            i.then_inc(h_done, 1)

                    def second_layer(e):
                        for k in range(KH):
                            pe.wait_ge(hT_ready, g * HU + e * KH + k + 1 + KH)
                            for j in range(tiles):
                                if k == 0:
                                    if e == 0:
                                        pe.wait_ge(b2_added, g + 1)
                                    else:
                                        pe.wait_ge(y_added, ybase + (e - 1) * tiles + j + 1)
                                i = three(ps_y[:, j, 0:D], hh[:, k, j * P:(j + 1) * P], hl[:, k, j * P:(j + 1) * P],
                                          w2h[:, e, k, :], w2l[:, e, k, :], k == 0, k == KH - 1)
                                if k == KH - 1:
                                    i.then_inc(y_done, 1)
                            if k < KH - 1:
                                i.then_inc(w2_done, 1)

                    first_layer(0)
                    for e in range(NX):
                        if e + 1 < NX:
                            first_layer(e + 1)
                        second_layer(e)

                groups(pe, body)


def kernel(**inputs):
    import concourse.bacc as bacc
    from concourse.bass_utils import run_bass_kernel_spmd

    a = {k: np.ascontiguousarray(v) for k, v in inputs.items()}
    x = np.zeros((NP_, D), np.float32)
    x[:N] = a["x"]
    src = np.zeros(EP, np.int32)
    src[:E] = a["src"]
    dst = np.full(EP, PAD_NODE, np.int32)
    dst[:E] = a["dst"]
    g = {k[len("L0_gnn_"):]: v for k, v in a.items() if k.startswith("L0_gnn_")}
    f = {k[len("L0_ffn_"):]: v for k, v in a.items() if k.startswith("L0_ffn_")}
    arrays = {
        "in_x": x,
        "in_src_idx": np.ascontiguousarray(src.reshape(NSUP, ET, P).transpose(0, 2, 1)),
        "in_dst_part": np.ascontiguousarray(dst.reshape(NSUP * ET, P).T),
        "in_dst_row": dst.reshape(NSUP, SUP),
        "in_W_src": g["W_src"], "in_W_dst": g["W_dst"],
        "in_att_src": g["att_src"].reshape(D), "in_att_dst": g["att_dst"].reshape(D),
        "in_bias": g["bias"], "in_ln_gamma": g["ln_gamma"], "in_ln_beta": g["ln_beta"], "in_prelu_w": g["prelu_w"],
        "in_Wg": f["Wg"], "in_bg": f["bg"], "in_gbias": f["bias"],
        "in_W1": f["W1"], "in_b1": f["b1"], "in_W2": f["W2"], "in_b2": f["b2"],
    }
    nc = bacc.Bacc("TRN2", target_bir_lowering=False, num_devices=1)
    args = [nc.dram_tensor(k, v.shape, mybir.dt.from_np(v.dtype), kind="ExternalInput").ap() for k, v in arrays.items()]
    args.append(nc.dram_tensor("out_x", (NP_, D), F32, kind="ExternalOutput").ap())
    build_program(nc, *args)
    r = run_bass_kernel_spmd(nc, [arrays], core_ids=[0])
    return r.results[0]["out_x"][:N]
```

```python
import numpy as np
import concourse.bass as bass
from concourse import mybir
from contextlib import ExitStack

F32 = mybir.dt.float32
F32R = mybir.dt.float32r
I32 = mybir.dt.int32
I16 = mybir.dt.int16
BF16 = mybir.dt.bfloat16
ALU = mybir.AluOpType
ACT = mybir.ActivationFunctionType
AX = mybir.AxisListType

P = 128
N, D = 6250, 256
E = 100000
HEADS, HC = 4, 64
NEG_SLOPE, LN_EPS = 0.2, 1e-5
TILES = -(-N // P)
NP_ = TILES * P
PAD_NODE = NP_ - 1
CH = 7
CHUNKS = TILES // CH
ET = 8
SUP = ET * P
NSUP = -(-E // SUP)
EP = NSUP * SUP
ROW = D + HEADS
KD = D // P
NX, HID = 8, 512
KH = HID // P
GT = 4
GROUPS = TILES // GT
PARTS = 3
SLOTS = 4
TINY = 1e-30

assert TILES % CH == 0 and NSUP % SLOTS == 2 and TILES - GROUPS * GT == 1


def hold(engine, semaphore, value, passed):
    engine.wait_ge(semaphore, value)
    engine.sem_inc(passed, 1)


def build_program(nc, x, src_idx, dst_part, dst_row, W_src, W_dst, att_src, att_dst, bias, ln_gamma, ln_beta,
                  prelu_w, Wg, bg, gbias, W1, b1, W2, b2, out):
    x_tiles = x.rearrange("(t p) d -> p t d", p=P)
    out_tiles = out.rearrange("(t p) d -> p t d", p=P)
    table = nc.dram_tensor("h_src_table", [NP_, ROW], F32).ap()
    table_tiles = table.rearrange("(t p) c -> p t c", p=P)
    bounds_dram = nc.dram_tensor("bounds_dram", [NSUP, 2], I32).ap()
    dst16 = nc.dram_tensor("dst16", [NSUP, SUP], I16).ap()
    x1_dram = nc.dram_tensor("x1_dram", [NP_, D], F32).ap()
    x1_tiles = x1_dram.rearrange("(t p) d -> p t d", p=P)

    whole = ExitStack()
    with whole:
        def sb(name, shape, dt=F32, ctx=whole):
            return ctx.enter_context(nc.sbuf_tensor(name, shape, dt))

        def ps(name, shape, ctx):
            return ctx.enter_context(nc.psum_tensor(name, shape, F32))

        def sem(name):
            return whole.enter_context(nc.semaphore(name))

        ident = sb("ident", [P, P])
        eps = sb("eps", [P, 1])
        bounds = sb("bounds", [1, NSUP, 2], I32)
        bounds_in = sem("bounds_in")
        sp_passed, dve_passed, pe_passed, pool_passed = sem("sp_passed"), sem("dve_passed"), sem("pe_passed"), sem("pool_passed")

        acc_ctx = ExitStack()
        with acc_ctx:
            acc = sb("acc", [P, TILES + 1, ROW], F32, acc_ctx)
            edge_ctx = ExitStack()
            node_id = sb("node_id", [P, TILES + 1], F32, edge_ctx)
            col_id = sb("col_id", [P, P], F32, edge_ctx)
            node_parts = sb("node_parts", [P, TILES, PARTS * 2 * HEADS], BF16, edge_ctx)
            block_base = sb("block_base", [P, TILES + 1], F32, edge_ctx)
            dst_f = sb("dst_f", [P, NSUP * ET], F32, edge_ctx)

            with ExitStack() as c:
                xs = sb("xs", [P, TILES, D], F32, c)
                hs = sb("hs", [P, TILES, ROW], F32, c)
                xn = sb("xn", [P, CH, D], F32, c)
                xnT = sb("xnT", [P, CH, KD, P], F32, c)
                stats = sb("stats", [P, CH, 6], F32, c)
                meanvar = sb("meanvar", [P, CH, 2], F32, c)
                sd = sb("sd", [P, CH], F32, c)
                rstd = sb("rstd", [P, TILES], F32, c)
                nmr = sb("nmr", [P, TILES], F32, c)
                w_aug = sb("w_aug", [P, KD, D + 2 * HEADS], F32, c)
                w_dst = sb("w_dst", [P, KD, D], F32, c)
                att_b = sb("att_b", [P, 2, D], F32, c)
                prod = sb("prod", [P, KD, D], F32, c)
                node_tab = sb("node_tab", [P, TILES, 2 * HEADS], F32, c)
                left = sb("left", [P, TILES, 2 * HEADS], F32, c)
                dst_i = sb("dst_i", [P, NSUP * ET], I32, c)
                rows16 = sb("rows16", [NSUP, SUP], I16, c)
                gmax = sb("gmax", [P, HEADS], F32, c)
                gmax_all = sb("gmax_all", [P, HEADS], F32, c)
                shift_z = sb("shift_z", [P, TILES, HEADS], F32, c)
                rows = sb("rows", [NSUP, SUP], I32, c)
                lohi = sb("lohi", [NSUP, 2], F32, c)
                lohi_i = sb("lohi_i", [NSUP, 2], I32, c)
                node_id_i = sb("node_id_i", [P, TILES + 1], I32, c)
                col_id_i = sb("col_id_i", [P, P], I32, c)
                ps_T = ps("ps_T", [P, 2, 512], c)
                ps_h = ps("ps_h", [P, 2, 512], c)

                dst_in, rows16_ready, dst16_out = sem("dst_in"), sem("rows16_ready"), sem("dst16_out")
                x_in, w_in, rows_in, table_out = sem("x_in"), sem("w_in"), sem("rows_in"), sem("table_out")
                consts_i, consts = sem("consts_i"), sem("consts")
                stats_ready, sd_ready, rstd_ready = sem("stats_ready"), sem("sd_ready"), sem("rstd_ready")
                w_ready, xn_ready, xT_done, xT_ready = sem("w_ready"), sem("xn_ready"), sem("xT_done"), sem("xT_ready")
                h_done, h_out, gmax_ready, gmax_done = sem("h_done"), sem("h_out"), sem("gmax_ready"), sem("gmax_done")
                lohi_ready = sem("lohi_ready")

                block = c.enter_context(nc.Block())

                @block.sync
                def _(sp):
                    sp.dma_start(rows[:], dst_row).then_inc(rows_in, 16)
                    sp.dma_start(dst_i[:], dst_part).then_inc(dst_in, 16)
                    with sp.Fori(0, CHUNKS) as g:
                        sp.dma_start(xs[:, bass.ds(g * CH, CH), :], x_tiles[:, bass.ds(g * CH, CH), :]).then_inc(x_in, 16)
                        hold(sp, x_in, g * 16 + 16, sp_passed)
                    sp.wait_ge(rows16_ready, 1)
                    sp.dma_start(dst16, rows16[:]).then_inc(dst16_out, 16)
                    sp.wait_ge(dst16_out, 16)
                    hold(sp, lohi_ready, 1, sp_passed)
                    sp.dma_start(bounds_dram, lohi_i[:]).then_inc(bounds_in, 16)
                    hold(sp, bounds_in, 16, sp_passed)
                    sp.dma_start(bounds[:], bounds_dram[None, :, :]).then_inc(bounds_in, 16)
                    hold(sp, bounds_in, 32, sp_passed)
                    with sp.Fori(0, CHUNKS) as g:
                        hold(sp, h_out, g * CH + CH + 1, sp_passed)
                        sp.dma_start(table_tiles[:, bass.ds(g * CH, CH), :], hs[:, bass.ds(g * CH, CH), :]).then_inc(table_out, 16)
                    hold(sp, table_out, 16 * CHUNKS, sp_passed)

                @block.scalar
                def _(act):
                    act.dma_start(w_aug[:, :, 0:D], W_src.rearrange("(k p) n -> p k n", p=P)).then_inc(w_in, 16)
                    act.dma_start(w_dst[:], W_dst.rearrange("(k p) n -> p k n", p=P)).then_inc(w_in, 16)
                    act.dma_start(att_b[:, 0, :], att_src.partition_broadcast(P)).then_inc(w_in, 16)
                    act.dma_start(att_b[:, 1, :], att_dst.partition_broadcast(P)).then_inc(w_in, 16)
                    act.wait_ge(consts, 1)
                    with act.Fori(0, CHUNKS) as g:
                        act.wait_ge(stats_ready, g + 1)
                        nc.scalar.activation(sd[:], meanvar[:, :, 1], ACT.Sqrt,
                                             bias=eps[:]).then_inc(sd_ready, 1)
                    with act.Fori(0, CHUNKS) as g:
                        act.wait_ge(rstd_ready, g + 1)
                        for j in range(CH):
                            t = g * CH + j
                            act.wait_ge(xT_done, t + 1)
                            nc.scalar.activation(xn[:, j, :], xs[:, bass.ds(t, 1), :], ACT.Identity,
                                                 bias=nmr[:, bass.ds(t, 1)], scale=rstd[:, bass.ds(t, 1)]).then_inc(xn_ready, 1)
                            act.wait_ge(xT_done, t + CH + 1)
                            act.wait_ge(h_done, t + 1)
                            nc.scalar.copy(xnT[:, j, :, :], ps_T[:, j % 2, 0:D]).then_inc(xT_ready, 1)

                @block.gpsimd
                def _(pool):
                    nc.gpsimd.memset(ident[:], 0.0)
                    nc.gpsimd.memset(eps[:], LN_EPS)
                    nc.gpsimd.iota(node_id_i[:], pattern=[[P, TILES + 1]], base=0, channel_multiplier=1)
                    nc.gpsimd.iota(col_id_i[:], pattern=[[1, P]], base=0, channel_multiplier=0)
                    pool.drain()
                    nc.gpsimd.tensor_copy(node_id[:], node_id_i[:])
                    nc.gpsimd.tensor_copy(col_id[:], col_id_i[:])
                    nc.gpsimd.affine_select(out=ident[:], in_=ident[:], compare_op=ALU.not_equal, fill=1.0, base=0,
                                            pattern=[[-1, P]], channel_multiplier=1)
                    pool.drain()
                    nc.gpsimd.memset(gmax_all[:], 0.0).then_inc(consts, 1)
                    nc.gpsimd.memset(acc[:], 0.0)
                    pool.wait_ge(consts, 1)
                    pool.wait_ge(gmax_ready, 1)
                    nc.gpsimd.partition_all_reduce(gmax_all[:], gmax[:], P, bass.bass_isa.ReduceOp.max).then_inc(gmax_done, 1)

                @block.vector
                def _(dve):
                    dve.sem_inc(h_out, 1)
                    dve.wait_ge(w_in, 64)
                    for side, w in ((0, w_aug[:, :, 0:D]), (1, w_dst[:])):
                        nc.vector.tensor_tensor(prod[:], w, att_b[:, side, :].unsqueeze(1).to_broadcast([P, KD, D]), ALU.mult)
                        dve.drain()
                        lo = D + side * HEADS
                        nc.vector.tensor_reduce(w_aug[:, :, lo:lo + HEADS], prod[:].rearrange("p k (h c) -> p k h c", h=HEADS),
                                                AX.X, ALU.add)
                        dve.drain()
                    nc.vector.memset(gmax[:], 0.0).then_inc(w_ready, 1)
                    dve.wait_ge(rows_in, 16)
                    nc.vector.tensor_reduce(lohi[:, 0:1], rows[:], AX.X, ALU.min)
                    nc.vector.tensor_reduce(lohi[:, 1:2], rows[:], AX.X, ALU.max)
                    dve.drain()
                    nc.vector.tensor_copy(lohi_i[:], lohi[:])
                    dve.drain()
                    nc.vector.tensor_scalar(lohi_i[:], lohi_i[:], 7, None, ALU.arith_shift_right)
                    dve.drain()
                    nc.vector.tensor_scalar(lohi_i[:, 1:2], lohi_i[:, 1:2], 1, None, ALU.add).then_inc(lohi_ready, 1)
                    nc.vector.tensor_copy(rows16[:], rows[:]).then_inc(rows16_ready, 1)
                    dve.wait_ge(dst_in, 16)
                    nc.vector.tensor_copy(dst_f[:], dst_i[:])
                    dve.wait_ge(consts, 1)
                    nc.vector.tensor_scalar(block_base[:], node_id[:], node_id[:, 0:1], None, ALU.subtract)
                    with dve.Fori(0, CHUNKS) as g:
                        dve.wait_ge(x_in, g * 16 + 16)
                        for j in range(CH):
                            nc.vector.bn_stats(stats[:, j, :], xs[:, bass.ds(g * CH + j, 1), :])
                        dve.drain()
                        for j in range(CH):
                            i = nc.vector.bn_aggr(meanvar[:, j, :], stats[:, j, :])
                        i.then_inc(stats_ready, 1)
                        dve.wait_ge(sd_ready, g + 1)
                        nc.vector.reciprocal(rstd[:, bass.ds(g * CH, CH)], sd[:])
                        dve.drain()
                        nc.vector.scalar_tensor_tensor(out=nmr[:, bass.ds(g * CH, CH)], in0=meanvar[:, :, 0],
                                                       scalar=-1.0, in1=rstd[:, bass.ds(g * CH, CH)], op0=ALU.mult,
                                                       op1=ALU.mult).then_inc(rstd_ready, 1)
                    with dve.Fori(0, CHUNKS) as g:
                        for j in range(CH):
                            t = g * CH + j
                            dve.wait_ge(h_done, t + CH + 1)
                            nc.vector.tensor_copy(hs[:, bass.ds(t, 1), :], ps_h[:, j % 2, 0:ROW])
                            nc.vector.tensor_copy(node_tab[:, bass.ds(t, 1), 0:HEADS],
                                                  ps_h[:, j % 2, ROW:ROW + HEADS]).then_inc(h_out, 1)
                    dve.drain()
                    nc.vector.tensor_reduce(gmax[:], hs[:, :, D:ROW].rearrange("p t h -> p h t"), AX.X, ALU.max).then_inc(gmax_ready, 1)
                    dve.wait_ge(gmax_done, 1)
                    nc.vector.tensor_tensor(shift_z[:], node_tab[:, :, 0:HEADS],
                                            gmax_all[:].unsqueeze(1).to_broadcast([P, TILES, HEADS]), ALU.add)
                    dve.drain()
                    nc.vector.scalar_tensor_tensor(out=node_tab[:, :, HEADS:2 * HEADS], in0=shift_z[:], scalar=NEG_SLOPE,
                                                   in1=shift_z[:], op0=ALU.mult, op1=ALU.max)
                    dve.drain()
                    part = [node_parts[:, :, k * 2 * HEADS:(k + 1) * 2 * HEADS] for k in range(PARTS)]
                    nc.vector.tensor_copy(part[0], node_tab[:])
                    dve.drain()
                    nc.vector.tensor_tensor(left[:], node_tab[:], part[0], ALU.subtract)
                    dve.drain()
                    nc.vector.tensor_copy(part[1], left[:])
                    dve.drain()
                    nc.vector.tensor_tensor(part[2], left[:], part[1], ALU.subtract)

                @block.tensor
                def _(pe):
                    pe.sem_inc(xT_done, CH)
                    pe.sem_inc(h_done, CH)
                    pe.wait_ge(consts, 1)
                    pe.wait_ge(w_ready, 1)
                    with pe.Fori(0, CHUNKS) as g:
                        for j in range(CH):
                            t = g * CH + j
                            pe.wait_ge(xn_ready, t + 1)
                            for k in range(KD):
                                i = nc.tensor.transpose(ps_T[:, j % 2, k * P:(k + 1) * P], xn[:, j, k * P:(k + 1) * P], ident[:])
                            i.then_inc(xT_done, 1)
                            pe.wait_ge(xT_ready, t + 1)
                            pe.wait_ge(h_out, t + 1 if j == 0 else t)
                            for k in range(KD):
                                i = nc.tensor.matmul(ps_h[:, j % 2, 0:D + 2 * HEADS], xnT[:, j, k, :], w_aug[:, k, :],
                                                     start=(k == 0), stop=(k == KD - 1))
                            i.then_inc(h_done, 1)

            with edge_ctx:
                with ExitStack() as c:
                    msg = sb("msg", [P, SLOTS, ET, ROW], F32, c)
                    idx = sb("idx", [P, SLOTS, ET], I32, c)
                    row_b = sb("row_b", [P, 2, SUP], I16, c)
                    sel_n = sb("sel_n", [P, 2, 2, 2, SUP // 2], BF16, c)
                    sel_e = sb("sel_e", [P, 3, 2, ET // 2, P], F32, c)
                    edge_tab = sb("edge_tab", [P, ET, 2 * HEADS], F32, c)
                    score = sb("score", [P, 2, ET, HEADS], F32, c)
                    zeros = sb("zeros", [1, PARTS * ET * 2 * HEADS], BF16, c)
                    ps_tab = ps("ps_tab", [P, 2, 512], c)
                    ps_agg = ps("ps_agg", [P, 3, 512], c)
                    idx_in = [sem(f"idx_in{u}") for u in range(SLOTS)]
                    gathered = [sem(f"gathered{u}") for u in range(SLOTS)]
                    row_in = [sem(f"row_in{u}") for u in range(2)]
                    row_used, zeros_ready = sem("row_used"), sem("zeros_ready")
                    seln_ready = [sem(f"seln_ready{h}") for h in range(2)]
                    tab_done, tab_out = sem("tab_done"), sem("tab_out")
                    score_ready, p_ready, msg_ready, msg_used = sem("score_ready"), sem("p_ready"), sem("msg_ready"), sem("msg_used")
                    sele_ready = [sem(f"sele_ready{h}") for h in range(2)]
                    seln_used, agg_done = sem("seln_used"), sem("agg_done")
                    block = c.enter_context(nc.Block())
                    HALF = ET // 2
                    TURNS = (NSUP - 2) // SLOTS

                    def steps(engine, step):
                        with engine.Fori(0, TURNS) as i:
                            for u in range(SLOTS):
                                step(i * SLOTS + u, u, i, 2)
                        for u in range(2):
                            step(TURNS * SLOTS + u, u, TURNS, 1 - u)

                    def ahead(s, u, i, k):
                        return s + k, (u + k) % SLOTS, i + (u + k) // SLOTS

                    def load_bounds(engine, regs, s):
                        engine.load(regs, bounds[0:1, bass.ds(s, 1), :] if not isinstance(s, int) else bounds[0:1, s, :])

                    def block_range(engine, regs):
                        return engine.snap(regs[0], min_val=0, max_val=TILES - 1), engine.snap(regs[1], min_val=1, max_val=TILES)

                    @block.sync
                    def _(sp):
                        for u in range(SLOTS):
                            sp.dma_start(idx[:, u, :], src_idx[u]).then_inc(idx_in[u], 16)
                        for u in range(2):
                            sp.dma_start(row_b[:, u, :], dst16[u:u + 1, :].partition_broadcast(P)).then_inc(row_in[u], 16)
                        with sp.Fori(0, (NSUP - SLOTS - 2) // SLOTS) as i:
                            for u in range(SLOTS):
                                s = i * SLOTS + u
                                hold(sp, row_used, s + 1, sp_passed)
                                sp.dma_start(row_b[:, u % 2, :], dst16[bass.ds(s + 2, 1), :].partition_broadcast(P)).then_inc(row_in[u % 2], 16)
                                hold(sp, gathered[u], i * (16 * ET) + 16 * ET, sp_passed)
                                sp.dma_start(idx[:, u, :], src_idx[bass.ds(s + SLOTS, 1)].rearrange("a p r -> (a p) r")).then_inc(idx_in[u], 16)
                        for s in range(NSUP - SLOTS - 2, NSUP - 2):
                            sp.wait_ge(row_used, s + 1)
                            sp.dma_start(row_b[:, s % 2, :], dst16[s + 2:s + 3, :].partition_broadcast(P)).then_inc(row_in[s % 2], 16)
                            if s + SLOTS < NSUP:
                                sp.wait_ge(gathered[s % SLOTS], (s // SLOTS + 1) * 16 * ET)
                                sp.dma_start(idx[:, s % SLOTS, :], src_idx[s + SLOTS]).then_inc(idx_in[s % SLOTS], 16)

                    @block.gpsimd
                    def _(pool):
                        def step(s, u, i, behind):
                            pool.wait_ge(idx_in[u], i * 16 + 16)
                            hold(pool, msg_used, s + 1, pool_passed)
                            for r in range(ET):
                                nc.gpsimd.indirect_dma_start(
                                    out=msg[:, u, r, :], out_offset=None, in_=table,
                                    in_offset=bass.IndirectOffsetOnAxis(ap=idx[:, u, r:r + 1], axis=0)
                                ).then_inc(gathered[u], 16)
                        steps(pool, step)

                    @block.scalar
                    def _(act):
                        def weigh(s, u):
                            act.wait_ge(score_ready, s + 1)
                            nc.scalar.activation(msg[:, u, :, D:ROW], score[:, u % 2, :, :], ACT.Exp).then_inc(p_ready, 1)

                        def step(s, u, i, behind):
                            if behind == 2:
                                weigh(*ahead(s, u, i, 2)[:2])
                        weigh(0, 0)
                        weigh(1, 1)
                        steps(act, step)

                    @block.vector
                    def _(dve):
                        dve.sem_inc(msg_used, SLOTS - 1)
                        nc.vector.memset(zeros[:], 0.0)
                        nc.vector.memset(ps_agg[:], 0.0)
                        dve.drain().then_inc(zeros_ready, 1)
                        npair, added, b_prev, bank_prev = (dve.alloc_register(n) for n in ("npair", "added", "b_prev", "bank_prev"))
                        now, nxt, then = ([dve.alloc_register(f"{n}{k}") for k in range(2)] for n in ("now", "next", "then"))
                        dve.reg_mov(npair, 0)
                        dve.reg_mov(added, 0)
                        dve.reg_mov(b_prev, TILES)
                        dve.reg_mov(bank_prev, 1)

                        def select_nodes(s, u, i, regs):
                            lo, end = block_range(dve, regs)

                            def select(b, slot):
                                for h in range(2):
                                    nc.vector.tensor_scalar(sel_n[:, u % 2, slot, h, :], row_b[:, u % 2, h * (SUP // 2):(h + 1) * (SUP // 2)],
                                                            node_id[:, bass.ds(b, 1)], None, ALU.is_equal).then_inc(seln_ready[h], 1)
                                dve.reg_add(npair, npair, 1)

                            hold(dve, row_in[u % 2], (s // 2 if isinstance(s, int) else i * (SLOTS // 2) + u // 2) * 16 + 16, dve_passed)
                            select(lo, 0)
                            with dve.If(end > lo + 1):
                                select(lo + 1, 1)
                            with dve.If(end > lo + 2):
                                with dve.Fori(lo + 2, end) as b:
                                    hold(dve, seln_used, dve.snap(npair), dve_passed)
                                    select(b, 1)
                            dve.drain().then_inc(row_used, 1)

                        def scores(s, u, i):
                            sc = score[:, u % 2, :, :]
                            dve.wait_ge(tab_done, s + 1)
                            nc.vector.tensor_reduce(edge_tab[:], ps_tab[:, u % 2, 0:PARTS * ET * 2 * HEADS].rearrange(
                                "p (r k c) -> p r c k", r=ET, k=PARTS), AX.X, ALU.add).then_inc(tab_out, 1)
                            dve.drain()
                            dve.wait_ge(gathered[u], i * (16 * ET) + 16 * ET)
                            nc.vector.tensor_tensor(sc, msg[:, u, :, D:ROW], edge_tab[:, :, 0:HEADS], ALU.add)
                            dve.drain()
                            nc.vector.scalar_tensor_tensor(out=sc, in0=sc, scalar=NEG_SLOPE, in1=sc, op0=ALU.mult, op1=ALU.max)
                            dve.drain()
                            nc.vector.tensor_tensor(sc, sc, edge_tab[:, :, HEADS:2 * HEADS], ALU.subtract).then_inc(score_ready, 1)

                        def weigh(s, u):
                            dve.wait_ge(p_ready, s + 1)
                            h4 = msg[:, u, :, 0:D].rearrange("p r (h c) -> p r h c", h=HEADS)
                            nc.vector.tensor_tensor(h4, h4, msg[:, u, :, D:ROW].unsqueeze(3).to_broadcast([P, ET, HEADS, HC]),
                                                    ALU.mult).then_inc(msg_ready, 1)

                        def add_last():
                            dve.wait_ge(agg_done, dve.snap(added) + 1)
                            b = dve.snap(b_prev, min_val=0, max_val=TILES)
                            bank = dve.snap(bank_prev, min_val=0, max_val=2)
                            return nc.vector.tensor_tensor(acc[:, bass.ds(b, 1), :], acc[:, bass.ds(b, 1), :],
                                                           ps_agg[:, bass.ds(bank, 1), 0:ROW], ALU.add)

                        def pending(b, bank):
                            dve.reg_add(added, added, 1)
                            dve.reg_mov(b_prev, b)
                            dve.reg_mov(bank_prev, bank)

                        def step(s, u, i, behind):
                            if behind == 2:
                                load_bounds(dve, then, s + 2)
                                select_nodes(*ahead(s, u, i, 2), then)

                            def select(b, slot):
                                for h in range(2):
                                    dst = dst_f[:, bass.ds(s * ET + h * HALF, HALF)]
                                    nc.vector.scalar_tensor_tensor(
                                        out=sel_e[:, slot, h, :, :], in0=col_id[:].unsqueeze(1).to_broadcast([P, HALF, P]),
                                        scalar=block_base[:, bass.ds(b, 1)], in1=dst.unsqueeze(2).to_broadcast([P, HALF, P]),
                                        op0=ALU.add, op1=ALU.is_equal).then_inc(sele_ready[h], 1)

                            lo, end = block_range(dve, now)
                            select(lo, u % 2)
                            add_last().then_inc(msg_used, 1)
                            pending(lo, u % 2)
                            with dve.If(end > lo + 1):
                                select(lo + 1, 2)
                            if behind >= 1:
                                weigh(*ahead(s, u, i, 1)[:2])
                            if behind == 2:
                                scores(*ahead(s, u, i, 2))
                            with dve.If(end > lo + 1):
                                dve.drain()
                                add_last()
                                pending(lo + 1, 2)
                            with dve.If(end > lo + 2):
                                with dve.Fori(lo + 2, end) as b:
                                    dve.drain()
                                    add_last()
                                    select(b, 2)
                                    pending(b, 2)
                            for k in range(2):
                                dve.reg_mov(now[k], nxt[k])
                                dve.reg_mov(nxt[k], then[k])

                        load_bounds(dve, now, 0)
                        load_bounds(dve, nxt, 1)
                        select_nodes(0, 0, 0, now)
                        select_nodes(1, 1, 0, nxt)
                        scores(0, 0, 0)
                        dve.drain()
                        weigh(0, 0)
                        scores(1, 1, 0)
                        steps(dve, step)
                        dve.drain()
                        add_last()

                    @block.tensor
                    def _(pe):
                        pe.sem_inc(agg_done, 1)
                        pe.sem_inc(tab_out, 2)
                        pe.wait_ge(zeros_ready, 1)
                        npair, epair = pe.alloc_register("npair"), pe.alloc_register("epair")
                        now, nxt, then = ([pe.alloc_register(f"{n}{k}") for k in range(2)] for n in ("now", "next", "then"))
                        pe.reg_mov(npair, 0)
                        pe.reg_mov(epair, 0)
                        W = PARTS * 2 * HEADS

                        def tables(s, u, regs):
                            lo, end = block_range(pe, regs)
                            pe.wait_ge(tab_out, s + 1)
                            bank = ps_tab[:, u % 2, 0:ET * W]
                            nc.tensor.matmul(bank, zeros[:, 0:P], zeros[:], start=True, stop=False)

                            def look_up(b, slot):
                                pe.reg_add(npair, npair, 1)
                                n = pe.snap(npair)
                                for h in range(2):
                                    pe.wait_ge(seln_ready[h], n)
                                    for r in range(HALF):
                                        at = (h * HALF + r) * W
                                        m = nc.tensor.matmul(bank[:, at:at + W], sel_n[:, u % 2, slot, h, r * P:(r + 1) * P],
                                                             node_parts[:, bass.ds(b, 1), :], start=False, stop=False)
                                m.then_inc(seln_used, 1)

                            look_up(lo, 0)
                            with pe.If(end > lo + 1):
                                with pe.Fori(lo + 1, end) as b:
                                    look_up(b, 1)
                            nc.tensor.matmul(bank, zeros[:, 0:P], zeros[:], start=False, stop=True).then_inc(tab_done, 1)

                        def step(s, u, i, behind):
                            if behind == 2:
                                load_bounds(pe, then, s + 2)
                                tables(*ahead(s, u, i, 2)[:2], then)
                            hold(pe, msg_ready, s + 1, pe_passed)
                            lo, end = block_range(pe, now)

                            def sum_up(slot):
                                pe.reg_add(epair, epair, 1)
                                n = pe.snap(epair)
                                for h in range(2):
                                    pe.wait_ge(sele_ready[h], n)
                                    for r in range(HALF):
                                        m = nc.tensor.matmul(ps_agg[:, slot, 0:ROW], sel_e[:, slot, h, r, :], msg[:, u, h * HALF + r, :],
                                                             start=(h + r == 0), stop=(h * HALF + r == ET - 1))
                                m.then_inc(agg_done, 1)

                            sum_up(u % 2)
                            with pe.If(end > lo + 1):
                                with pe.Fori(lo + 1, end) as b:
                                    sum_up(2)
                            for k in range(2):
                                pe.reg_mov(now[k], nxt[k])
                                pe.reg_mov(nxt[k], then[k])

                        load_bounds(pe, now, 0)
                        load_bounds(pe, nxt, 1)
                        tables(0, 0, now)
                        tables(1, 1, nxt)
                        steps(pe, step)

                with ExitStack() as c:
                    xr = sb("xr", [P, CH, D], F32, c)
                    o = sb("o", [P, CH, D], F32, c)
                    pos = sb("pos", [P, CH, D], F32, c)
                    x1 = sb("x1", [P, CH, D], F32, c)
                    rden = sb("rden", [P, TILES, HEADS], F32, c)
                    vec = sb("vec", [P, 4, D], F32, c)
                    stats = sb("stats4", [P, CH, 6], F32, c)
                    meanvar = sb("meanvar4", [P, CH, 2], F32, c)
                    sd = sb("sd4", [P, CH], F32, c)
                    rstd = sb("rstd4", [P, CH], F32, c)
                    nmr = sb("nmr4", [P, CH], F32, c)
                    vec_in, xr_in, x1_stored = sem("vec_in"), sem("xr_in"), sem("x1_stored")
                    stats_ready, sd_ready, rstd_ready = sem("stats4_ready"), sem("sd4_ready"), sem("rstd4_ready")
                    norm_ready, y_ready, pos_ready, x1_ready, x_added = sem("norm4_ready"), sem("y4_ready"), sem("pos4_ready"), sem("x1_ready"), sem("x4_added")
                    block = c.enter_context(nc.Block())

                    def row(k):
                        return vec[:, k, :].unsqueeze(1).to_broadcast([P, CH, D])

                    @block.sync
                    def _(sp):
                        for k, v in enumerate((bias, ln_gamma, ln_beta, prelu_w)):
                            sp.dma_start(vec[:, k, :], v.partition_broadcast(P)).then_inc(vec_in, 16)
                        with sp.Fori(0, CHUNKS) as g:
                            hold(sp, x1_ready, g + 1, sp_passed)
                            sp.dma_start(xr[:], x_tiles[:, bass.ds(g * CH, CH), :]).then_inc(xr_in, 16)
                            hold(sp, x1_ready, g + 2, sp_passed)
                            sp.dma_start(x1_tiles[:, bass.ds(g * CH, CH), :], x1[:]).then_inc(x1_stored, 16)
                            hold(sp, x1_stored, 16 * g + 32, sp_passed)

                    @block.gpsimd
                    def _(pool):
                        with pool.Fori(0, CHUNKS) as g:
                            pool.wait_ge(xr_in, 16 * g + 16)
                            pool.wait_ge(pos_ready, g + 1)
                            nc.gpsimd.tensor_tensor(xr[:], xr[:], pos[:], ALU.add).then_inc(x_added, 1)

                    @block.scalar
                    def _(act):
                        with act.Fori(0, CHUNKS) as g:
                            act.wait_ge(stats_ready, g + 1)
                            nc.scalar.activation(sd[:], meanvar[:, :, 1], ACT.Sqrt, bias=eps[:]).then_inc(sd_ready, 1)
                            act.wait_ge(rstd_ready, g + 1)
                            for j in range(CH):
                                i = nc.scalar.activation(o[:, j, :], o[:, j, :], ACT.Identity, bias=nmr[:, j:j + 1], scale=rstd[:, j:j + 1])
                            i.then_inc(norm_ready, 1)
                            act.wait_ge(y_ready, g + 1)
                            nc.scalar.activation(pos[:], o[:], ACT.Relu).then_inc(pos_ready, 1)

                    @block.vector
                    def _(dve):
                        dve.sem_inc(x1_ready, 1)
                        dve.sem_inc(x1_stored, 16)
                        nc.vector.tensor_scalar(rden[:], acc[:, 0:TILES, D:ROW], TINY, None, ALU.max)
                        dve.drain()
                        nc.vector.reciprocal(rden[:], rden[:])
                        dve.drain()
                        dve.wait_ge(vec_in, 64)
                        with dve.Fori(0, CHUNKS) as g:
                            dve.drain()
                            nc.vector.tensor_tensor(o[:].rearrange("p t (h c) -> p t h c", h=HEADS),
                                                    acc[:, bass.ds(g * CH, CH), 0:D].rearrange("p t (h c) -> p t h c", h=HEADS),
                                                    rden[:, bass.ds(g * CH, CH), :].unsqueeze(3).to_broadcast([P, CH, HEADS, HC]), ALU.mult)
                            dve.drain()
                            nc.vector.tensor_tensor(o[:], o[:], row(0), ALU.add)
                            dve.drain()
                            for j in range(CH):
                                nc.vector.bn_stats(stats[:, j, :], o[:, j, :])
                            dve.drain()
                            for j in range(CH):
                                i = nc.vector.bn_aggr(meanvar[:, j, :], stats[:, j, :])
                            i.then_inc(stats_ready, 1)
                            dve.wait_ge(sd_ready, g + 1)
                            nc.vector.reciprocal(rstd[:], sd[:])
                            dve.drain()
                            nc.vector.scalar_tensor_tensor(out=nmr[:], in0=meanvar[:, :, 0], scalar=-1.0, in1=rstd[:],
                                                           op0=ALU.mult, op1=ALU.mult).then_inc(rstd_ready, 1)
                            dve.wait_ge(norm_ready, g + 1)
                            nc.vector.tensor_tensor(o[:], o[:], row(1), ALU.mult)
                            dve.drain()
                            nc.vector.tensor_tensor(o[:], o[:], row(2), ALU.add).then_inc(y_ready, 1)
                            dve.wait_ge(pos_ready, g + 1)
                            nc.vector.scalar_tensor_tensor(out=o[:], in0=o[:], scalar=0.0, in1=row(3), op0=ALU.min, op1=ALU.mult)
                            dve.drain()
                            dve.wait_ge(x_added, g + 1)
                            dve.wait_ge(x1_stored, 16 * g + 16)
                            nc.vector.tensor_tensor(x1[:], xr[:], o[:], ALU.add).then_inc(x1_ready, 1)

        with ExitStack() as c:
            w1h = sb("w1h", [P, NX, KD, HID], F32R, c)
            w1l = sb("w1l", [P, NX, KD, HID], F32R, c)
            w2h = sb("w2h", [P, NX, KH, D], F32R, c)
            w2l = sb("w2l", [P, NX, KH, D], F32R, c)
            raw = sb("raw", [P, 2, KD * HID], F32, c)
            wgh = sb("wgh", [P, KD, NX], F32R, c)
            wgl = sb("wgl", [P, KD, NX], F32R, c)
            wg = sb("wg", [P, KD, NX], F32, c)
            gate_b = sb("gate_b", [P, 2, NX], F32, c)
            b1_rows = sb("b1_rows", [NX * KH, P], F32, c)
            b1T = sb("b1T", [P, NX * KH], F32, c)
            b2_sb = sb("b2_sb", [NX, D], F32, c)
            ramp_i = sb("ramp_i", [P, GT, NX], I32, c)
            ramp = sb("ramp", [P, GT, NX], F32, c)
            y = sb("y", [P, 2 * GT, D], F32, c)
            xn = sb("xn5", [P, GT, D], F32, c)
            xTh = sb("xTh", [P, KD, GT * P], F32R, c)
            xTl = sb("xTl", [P, KD, GT * P], F32R, c)
            h32 = sb("h32", [P, KH, GT * P], F32, c)
            hh = sb("hh", [P, KH, GT * P], F32R, c)
            hl = sb("hl", [P, KH, GT * P], F32R, c)
            stats = sb("stats5", [P, GT, 6], F32, c)
            meanvar = sb("meanvar5", [P, GT, 2], F32, c)
            sd = sb("sd5", [P, GT], F32, c)
            rstd = sb("rstd5", [P, GT], F32, c)
            nmr = sb("nmr5", [P, GT], F32, c)
            logit = sb("logit", [P, GT, NX], F32, c)
            work = sb("work", [P, GT, NX], F32, c)
            pick = sb("pick", [P, 2, GT, NX], F32, c)
            top = sb("top", [P, 2, GT], F32, c)
            first = sb("first", [P, GT], F32, c)
            gap = sb("gap", [P, GT], F32, c)
            wts = sb("wts", [P, 2, GT], F32, c)
            comb = sb("comb", [P, GT, NX], F32, c)
            combT = sb("combT", [NX, GT, P], F32, c)
            ps_h = ps("ps_h5", [P, KH, 512], c)
            ps_y = ps("ps_y5", [P, GT, 512], c)

            small_in, raw_in, raw_used = sem("small_in"), [sem("raw_in0"), sem("raw_in1")], sem("raw_used")
            ramp_ready, b1T_done, b1T_ready, weights_ready = sem("ramp_ready"), sem("b1T_done"), sem("b1T_ready"), sem("weights_ready")
            x1_in, y_out = sem("x1_in"), sem("y_out")
            stats_ready, sd_ready, rstd_ready = sem("stats5_ready"), sem("sd5_ready"), sem("rstd5_ready")
            xn_ready, xT_done, xh_ready, xl_ready = sem("xn5_ready"), sem("xT5_done"), sem("xh_ready"), sem("xl_ready")
            logit_done, gap_ready, e_ready = sem("logit_done"), sem("gap_ready"), sem("e_ready")
            comb_ready, combT_done, combT_ready, b2_done, b2_added = (sem("comb_ready"), sem("combT_done"), sem("combT_ready"),
                                                                      sem("b2_done"), sem("b2_added"))
            h_done, h_out, hT_ready, w2_done, y_done, y_added = (sem("h5_done"), sem("h5_out"), sem("hT_ready"), sem("w2_done"),
                                                                 sem("y5_done"), sem("y5_added"))
            HU = NX * KH
            block = c.enter_context(nc.Block())

            def groups(engine, body):
                with engine.Fori(0, GROUPS) as g:
                    body(g, g * GT, GT, (g % 2) * GT, g * (NX * GT))
                body(GROUPS, GROUPS * GT, 1, (GROUPS % 2) * GT, GROUPS * NX * GT)

            @block.sync
            def _(sp):
                sp.dma_start(wg[:], Wg.rearrange("(k p) n -> p k n", p=P)).then_inc(small_in, 16)
                sp.dma_start(gate_b[:, 0, :], bg.partition_broadcast(P)).then_inc(small_in, 16)
                sp.dma_start(gate_b[:, 1, :], gbias.partition_broadcast(P)).then_inc(small_in, 16)
                sp.dma_start(b1_rows[:], b1.rearrange("e (k p) -> (e k) p", p=P)).then_inc(small_in, 16)
                sp.dma_start(b2_sb[:], b2).then_inc(small_in, 16)
                for g in range(2):
                    sp.dma_start(y[:, g * GT:(g + 1) * GT, :], x1_tiles[:, g * GT:(g + 1) * GT, :]).then_inc(x1_in, 16)
                    hold(sp, x1_in, 16 * g + 16, sp_passed)
                with sp.Fori(0, NX) as e:
                    hold(sp, raw_used, 2 * e + 1, sp_passed)
                    sp.dma_start(raw[:, 0, :].rearrange("p (k n) -> p k n", k=KD),
                                 W1[bass.ds(e, 1)].rearrange("a (k p) n -> p (a k) n", p=P)).then_inc(raw_in[0], 16)
                    hold(sp, raw_used, 2 * e + 2, sp_passed)
                    sp.dma_start(raw[:, 1, :].rearrange("p (k n) -> p k n", k=KH),
                                 W2[bass.ds(e, 1)].rearrange("a (k p) n -> p (a k) n", p=P)).then_inc(raw_in[1], 16)

                def store(g, slot, tile, tiles):
                    sp.dma_start(out_tiles[:, bass.ds(tile, tiles), :] if not isinstance(tile, int) else out_tiles[:, tile:tile + tiles, :],
                                 y[:, bass.ds(slot, tiles), :] if not isinstance(slot, int) else y[:, slot:slot + tiles, :]
                                 ).then_inc(y_out, 16)
                    hold(sp, y_out, 16 * g + 16, sp_passed)

                with sp.Fori(0, GROUPS - 2) as g:
                    hold(sp, y_added, g * (NX * GT) + NX * GT, sp_passed)
                    store(g, (g % 2) * GT, g * GT, GT)
                    sp.dma_start(y[:, bass.ds((g % 2) * GT, GT), :], x1_tiles[:, bass.ds(g * GT + 2 * GT, GT), :]).then_inc(x1_in, 16)
                for g in (GROUPS - 2, GROUPS - 1):
                    hold(sp, y_added, (g + 1) * NX * GT, sp_passed)
                    store(g, (g % 2) * GT, g * GT, GT)
                    if g == GROUPS - 2:
                        slot = (GROUPS % 2) * GT
                        sp.dma_start(y[:, slot:slot + 1, :], x1_tiles[:, GROUPS * GT:TILES, :]).then_inc(x1_in, 16)
                hold(sp, y_added, GROUPS * NX * GT + NX, sp_passed)
                store(GROUPS, (GROUPS % 2) * GT, GROUPS * GT, 1)

            @block.gpsimd
            def _(pool):
                nc.gpsimd.iota(ramp_i[:], pattern=[[0, GT], [1, NX]], base=-NX, channel_multiplier=0)
                pool.drain()
                nc.gpsimd.tensor_copy(ramp[:], ramp_i[:]).then_inc(ramp_ready, 1)

            @block.scalar
            def _(act):
                act.wait_ge(b1T_done, 1)
                nc.scalar.copy(b1T[:], ps_y[:, 0, 0:NX * KH]).then_inc(b1T_ready, 1)

                def body(g, tile, tiles, slot, ybase):
                    cols = tiles * P
                    act.wait_ge(stats_ready, g + 1)
                    nc.scalar.activation(sd[:, 0:tiles], meanvar[:, 0:tiles, 1], ACT.Sqrt, bias=eps[:]).then_inc(sd_ready, 1)
                    act.wait_ge(rstd_ready, g + 1)
                    for j in range(tiles):
                        i = nc.scalar.activation(xn[:, j, :], y[:, bass.ds(slot + j, 1), :] if not isinstance(slot, int) else y[:, slot + j, :],
                                                 ACT.Identity, bias=nmr[:, j:j + 1], scale=rstd[:, j:j + 1])
                    i.then_inc(xn_ready, 1)
                    act.wait_ge(xT_done, g + 1)
                    for k in range(KD):
                        nc.scalar.copy(xTh[:, k, 0:cols], ps_h[:, k, 0:cols]).then_inc(xh_ready, 1)
                    act.wait_ge(gap_ready, g + 1)
                    nc.scalar.activation(wts[:, 1, 0:tiles], gap[:, 0:tiles], ACT.Exp).then_inc(e_ready, 1)
                    act.wait_ge(combT_done, g + 1)
                    nc.scalar.copy(combT[:, 0:tiles, :], ps_h[0:NX, 3, 0:cols]).then_inc(combT_ready, 1)
                    for n in range(HU):
                        act.wait_ge(h_done, g * HU + n + 1)
                        act.wait_ge(hT_ready, g * HU + n + 1)
                        nc.scalar.activation(h32[:, n % KH, 0:cols], ps_h[:, n % KH, 0:cols], ACT.Relu,
                                             bias=b1T[:, n:n + 1]).then_inc(h_out, 1)

                groups(act, body)

            @block.vector
            def _(dve):
                dve.sem_inc(hT_ready, KH)
                dve.sem_inc(raw_used, 2)
                dve.wait_ge(small_in, 80)
                nc.vector.tensor_copy(wgh[:], wg[:])
                nc.vector.tensor_tensor(gate_b[:, 0, :], gate_b[:, 0, :], gate_b[:, 1, :], ALU.add)
                dve.drain()
                nc.vector.tensor_tensor(wgl[:], wg[:], wgh[:].bitcast(F32), ALU.subtract)
                with dve.Fori(0, NX) as e:
                    for u, (hi, lo) in enumerate(((w1h, w1l), (w2h, w2l))):
                        hi_e = hi[:, bass.ds(e, 1)].rearrange("p a k n -> p (a k n)")
                        lo_e = lo[:, bass.ds(e, 1)].rearrange("p a k n -> p (a k n)")
                        dve.wait_ge(raw_in[u], 16 * e + 16)
                        nc.vector.tensor_copy(hi_e, raw[:, u, :])
                        dve.drain()
                        nc.vector.tensor_tensor(lo_e, raw[:, u, :], hi_e.bitcast(F32), ALU.subtract).then_inc(raw_used, 1)
                dve.drain().then_inc(weights_ready, 1)

                def body(g, tile, tiles, slot, ybase):
                    cols = tiles * P

                    def yt(j):
                        return y[:, slot + j, :] if isinstance(slot, int) else y[:, bass.ds(slot + j, 1), :].rearrange("p a d -> p (a d)")

                    dve.wait_ge(x1_in, 16 * g + 16)
                    for j in range(tiles):
                        nc.vector.bn_stats(stats[:, j, :], yt(j))
                    dve.drain()
                    for j in range(tiles):
                        i = nc.vector.bn_aggr(meanvar[:, j, :], stats[:, j, :])
                    i.then_inc(stats_ready, 1)
                    dve.wait_ge(sd_ready, g + 1)
                    nc.vector.reciprocal(rstd[:, 0:tiles], sd[:, 0:tiles])
                    dve.drain()
                    nc.vector.scalar_tensor_tensor(out=nmr[:, 0:tiles], in0=meanvar[:, 0:tiles, 0], scalar=-1.0, in1=rstd[:, 0:tiles],
                                                   op0=ALU.mult, op1=ALU.mult).then_inc(rstd_ready, 1)
                    for k in range(KD):
                        dve.wait_ge(xh_ready, g * KD + k + 1)
                        nc.vector.tensor_tensor(xTl[:, k, 0:cols], ps_h[:, k, 0:cols], xTh[:, k, 0:cols].bitcast(F32),
                                                ALU.subtract).then_inc(xl_ready, 1)
                    dve.wait_ge(logit_done, g + 1)
                    dve.wait_ge(ramp_ready, 1)
                    lg, wk, rp = logit[:, 0:tiles, :], work[:, 0:tiles, :], ramp[:, 0:tiles, :]

                    def wide(v):
                        return v.unsqueeze(2).to_broadcast([P, tiles, NX])

                    nc.vector.tensor_tensor(lg, ps_h[:, 2, 0:tiles * NX].rearrange("p (t e) -> p t e", e=NX),
                                            gate_b[:, 0, :].unsqueeze(1).to_broadcast([P, tiles, NX]), ALU.add)
                    dve.drain()
                    for q in range(2):
                        nc.vector.tensor_reduce(top[:, q, 0:tiles], lg, AX.X, ALU.max)
                        dve.drain()
                        nc.vector.tensor_tensor(wk, lg, wide(top[:, q, 0:tiles]), ALU.is_equal)
                        dve.drain()
                        nc.vector.tensor_tensor(wk, wk, rp, ALU.mult)
                        dve.drain()
                        nc.vector.tensor_reduce(first[:, 0:tiles], wk, AX.X, ALU.min)
                        dve.drain()
                        nc.vector.tensor_tensor(pick[:, q, 0:tiles, :], rp, wide(first[:, 0:tiles]), ALU.is_equal)
                        dve.drain()
                        if q == 0:
                            nc.vector.tensor_scalar(wk, pick[:, 0, 0:tiles, :], -3e38, None, ALU.mult)
                            dve.drain()
                            nc.vector.tensor_tensor(lg, lg, wk, ALU.add)
                            dve.drain()
                    nc.vector.tensor_tensor(gap[:, 0:tiles], top[:, 1, 0:tiles], top[:, 0, 0:tiles], ALU.subtract).then_inc(gap_ready, 1)
                    dve.wait_ge(e_ready, g + 1)
                    nc.vector.tensor_scalar(wts[:, 0, 0:tiles], wts[:, 1, 0:tiles], 1.0, None, ALU.add)
                    dve.drain()
                    nc.vector.reciprocal(wts[:, 0, 0:tiles], wts[:, 0, 0:tiles])
                    dve.drain()
                    nc.vector.tensor_tensor(wts[:, 1, 0:tiles], wts[:, 1, 0:tiles], wts[:, 0, 0:tiles], ALU.mult)
                    dve.drain()
                    for q in range(2):
                        pk = pick[:, q, 0:tiles, :]
                        nc.vector.tensor_tensor(pk, pk, wide(wts[:, q, 0:tiles]), ALU.mult)
                    dve.drain()
                    nc.vector.tensor_tensor(comb[:, 0:tiles, :], pick[:, 0, 0:tiles, :], pick[:, 1, 0:tiles, :], ALU.add).then_inc(comb_ready, 1)
                    for j in range(tiles):
                        if j == 0:
                            dve.wait_ge(b2_done, g + 1)
                        i = nc.vector.tensor_tensor(yt(j), yt(j), ps_y[:, j, 0:D], ALU.add)
                    i.then_inc(b2_added, 1)
                    dve.drain()

                    def split(e):
                        for k in range(KH):
                            n = e * KH + k
                            dve.wait_ge(h_out, g * HU + n + 1)
                            if k < KH - 1:
                                dve.wait_ge(w2_done, g * (NX * (KH - 1)) + e * (KH - 1) + k + 1)
                            else:
                                dve.wait_ge(y_done, ybase + e * tiles + 1)
                            nc.vector.tensor_copy(hh[:, k, 0:cols], h32[:, k, 0:cols])
                            dve.drain()
                            nc.vector.tensor_tensor(hl[:, k, 0:cols], h32[:, k, 0:cols], hh[:, k, 0:cols].bitcast(F32),
                                                    ALU.subtract).then_inc(hT_ready, 1)

                    split(0)
                    for e in range(NX):
                        if e + 1 < NX:
                            split(e + 1)
                        for j in range(tiles):
                            dve.wait_ge(y_done, ybase + e * tiles + j + 2)
                            nc.vector.scalar_tensor_tensor(out=yt(j), in0=ps_y[:, j, 0:D], scalar=comb[:, j, e:e + 1], in1=yt(j),
                                                           op0=ALU.mult, op1=ALU.add).then_inc(y_added, 1)

                groups(dve, body)

            @block.tensor
            def _(pe):
                pe.sem_inc(w2_done, KH - 1)
                pe.sem_inc(y_done, 1)
                pe.wait_ge(small_in, 80)
                nc.tensor.transpose(ps_y[:, 0, 0:NX * KH], b1_rows[:], ident[0:NX * KH, 0:NX * KH]).then_inc(b1T_done, 1)
                pe.wait_ge(b1T_ready, 1)
                pe.wait_ge(weights_ready, 1)

                def three(out_, ah, al, bh, bl, start, stop):
                    nc.tensor.matmul(out_, ah, bh, start=start, stop=False)
                    nc.tensor.matmul(out_, ah, bl, start=False, stop=False)
                    return nc.tensor.matmul(out_, al, bh, start=False, stop=stop)

                def body(g, tile, tiles, slot, ybase):
                    cols = tiles * P
                    pe.wait_ge(xn_ready, g + 1)
                    for k in range(KD):
                        for j in range(tiles):
                            i = nc.tensor.transpose(ps_h[:, k, j * P:(j + 1) * P], xn[:, j, k * P:(k + 1) * P], ident[:])
                    i.then_inc(xT_done, 1)
                    pe.wait_ge(xh_ready, g * KD + KD)
                    pe.wait_ge(xl_ready, g * KD + KD)
                    for j in range(tiles):
                        for k in range(KD):
                            i = three(ps_h[:, 2, j * NX:(j + 1) * NX], xTh[:, k, j * P:(j + 1) * P], xTl[:, k, j * P:(j + 1) * P],
                                      wgh[:, k, :], wgl[:, k, :], k == 0, k == KD - 1)
                    i.then_inc(logit_done, 1)
                    pe.wait_ge(comb_ready, g + 1)
                    for j in range(tiles):
                        i = nc.tensor.transpose(ps_h[0:NX, 3, j * P:(j + 1) * P], comb[:, j, :], ident[:])
                    i.then_inc(combT_done, 1)
                    pe.wait_ge(combT_ready, g + 1)
                    for j in range(tiles):
                        i = nc.tensor.matmul(ps_y[:, j, 0:D], combT[:, j, :], b2_sb[:], start=True, stop=True)
                    i.then_inc(b2_done, 1)

                    def first_layer(e):
                        for m in range(KH):
                            n = e * KH + m
                            if e > 0:
                                pe.wait_ge(h_out, g * HU + n - KH + 1)
                            for k in range(KD):
                                i = three(ps_h[:, m, 0:cols], w1h[:, e, k, m * P:(m + 1) * P], w1l[:, e, k, m * P:(m + 1) * P],
                                          xTh[:, k, 0:cols], xTl[:, k, 0:cols], k == 0, k == KD - 1)
                            i.then_inc(h_done, 1)

                    def second_layer(e):
                        for k in range(KH):
                            pe.wait_ge(hT_ready, g * HU + e * KH + k + 1 + KH)
                            for j in range(tiles):
                                if k == 0:
                                    if e == 0:
                                        pe.wait_ge(b2_added, g + 1)
                                    else:
                                        pe.wait_ge(y_added, ybase + (e - 1) * tiles + j + 1)
                                i = three(ps_y[:, j, 0:D], hh[:, k, j * P:(j + 1) * P], hl[:, k, j * P:(j + 1) * P],
                                          w2h[:, e, k, :], w2l[:, e, k, :], k == 0, k == KH - 1)
                                if k == KH - 1:
                                    i.then_inc(y_done, 1)
                            if k < KH - 1:
                                i.then_inc(w2_done, 1)

                    first_layer(0)
                    for e in range(NX):
                        if e + 1 < NX:
                            first_layer(e + 1)
                        second_layer(e)

                groups(pe, body)


def kernel(**inputs):
    import concourse.bacc as bacc
    from concourse.bass_utils import run_bass_kernel_spmd

    a = {k: np.ascontiguousarray(v) for k, v in inputs.items()}
    x = np.zeros((NP_, D), np.float32)
    x[:N] = a["x"]
    src = np.zeros(EP, np.int32)
    src[:E] = a["src"]
    dst = np.full(EP, PAD_NODE, np.int32)
    dst[:E] = a["dst"]
    g = {k[len("L0_gnn_"):]: v for k, v in a.items() if k.startswith("L0_gnn_")}
    f = {k[len("L0_ffn_"):]: v for k, v in a.items() if k.startswith("L0_ffn_")}
    arrays = {
        "in_x": x,
        "in_src_idx": np.ascontiguousarray(src.reshape(NSUP, ET, P).transpose(0, 2, 1)),
        "in_dst_part": np.ascontiguousarray(dst.reshape(NSUP * ET, P).T),
        "in_dst_row": dst.reshape(NSUP, SUP),
        "in_W_src": g["W_src"], "in_W_dst": g["W_dst"],
        "in_att_src": g["att_src"].reshape(D), "in_att_dst": g["att_dst"].reshape(D),
        "in_bias": g["bias"], "in_ln_gamma": g["ln_gamma"], "in_ln_beta": g["ln_beta"], "in_prelu_w": g["prelu_w"],
        "in_Wg": f["Wg"], "in_bg": f["bg"], "in_gbias": f["bias"],
        "in_W1": f["W1"], "in_b1": f["b1"], "in_W2": f["W2"], "in_b2": f["b2"],
    }
    nc = bacc.Bacc("TRN2", target_bir_lowering=False, num_devices=1)
    args = [nc.dram_tensor(k, v.shape, mybir.dt.from_np(v.dtype), kind="ExternalInput").ap() for k, v in arrays.items()]
    args.append(nc.dram_tensor("out_x", (NP_, D), F32, kind="ExternalOutput").ap())
    build_program(nc, *args)
    r = run_bass_kernel_spmd(nc, [arrays], core_ids=[0])
    return r.results[0]["out_x"][:N]
```

```python
import numpy as np
import concourse.bass as bass
from concourse import mybir
from contextlib import ExitStack

F32 = mybir.dt.float32
F32R = mybir.dt.float32r
I32 = mybir.dt.int32
I16 = mybir.dt.int16
BF16 = mybir.dt.bfloat16
ALU = mybir.AluOpType
ACT = mybir.ActivationFunctionType
AX = mybir.AxisListType

P = 128
N, D = 6250, 256
E = 100000
HEADS, HC = 4, 64
NEG_SLOPE, LN_EPS = 0.2, 1e-5
TILES = -(-N // P)
NP_ = TILES * P
PAD_NODE = NP_ - 1
CH = 7
CHUNKS = TILES // CH
ET = 8
SUP = ET * P
NSUP = -(-E // SUP)
EP = NSUP * SUP
ROW = D + HEADS
KD = D // P
NX, HID = 8, 512
KH = HID // P
GT = 4
GROUPS = TILES // GT
ROOT_GUESS, NEWTON = float(0x5f3759df), 3
HB, TB = 4, 4
YB = 2
YC = GT + 1
PARTS = 3
SLOTS = 6
TINY = 1e-30
MAX_SPREAD = 40.0
LOWEST = -1e30

assert TILES % CH == 0 and NSUP % SLOTS == 2 and TILES - GROUPS * GT == 1


def hold(engine, semaphore, value, passed):
    engine.wait_ge(semaphore, value)
    engine.sem_inc(passed, 1)


def inverse_root(nc, variance, roots, root_i, result):
    v, half_v, square = roots[:, 0, :], roots[:, 1, :], roots[:, 2, :]
    dve = nc.vector
    dve.tensor_scalar(v, variance, LN_EPS, None, ALU.add)
    dve.tensor_scalar(half_v, variance, LN_EPS, -0.5, ALU.add, ALU.mult)
    dve.drain()
    dve.tensor_scalar(root_i[:], v.bitcast(I32), 1, None, ALU.arith_shift_right)
    dve.drain()
    dve.tensor_scalar(root_i[:], root_i[:], -1.0, ROOT_GUESS, ALU.mult, ALU.add)
    dve.drain()
    root = root_i[:].bitcast(F32)
    for k in range(NEWTON):
        dve.tensor_tensor(square, root, root, ALU.mult)
        dve.drain()
        dve.tensor_tensor(square, square, half_v, ALU.mult)
        dve.drain()
        dve.scalar_tensor_tensor(out=result if k == NEWTON - 1 else root, in0=square, scalar=1.5, in1=root, op0=ALU.add, op1=ALU.mult)
        dve.drain()


def build_program(nc, x, src_idx, dst_part, dst_row, W_src, W_dst, att_src, att_dst, bias, ln_gamma, ln_beta,
                  prelu_w, Wg, bg, gbias, W1, b1, W2, b2, out):
    x_tiles = x.rearrange("(t p) d -> p t d", p=P)
    out_tiles = out.rearrange("(t p) d -> p t d", p=P)
    table = nc.dram_tensor("h_src_table", [NP_, ROW], F32).ap()
    table_tiles = table.rearrange("(t p) c -> p t c", p=P)
    bounds_dram = nc.dram_tensor("bounds_dram", [NSUP, 2], I32).ap()
    dst16 = nc.dram_tensor("dst16", [NSUP, SUP], I16).ap()
    sums_dram = nc.dram_tensor("sums_dram", [NP_, ROW], F32).ap()
    sums_tiles = sums_dram.rearrange("(t p) c -> p t c", p=P)

    assert GT * P == HID
    with ExitStack() as whole:
        def sb(name, shape, dt=F32, ctx=whole):
            return ctx.enter_context(nc.sbuf_tensor(name, shape, dt))

        def ps(name, shape, ctx):
            return ctx.enter_context(nc.psum_tensor(name, shape, F32))

        def sem(name):
            return whole.enter_context(nc.semaphore(name))

        ident = sb("ident", [P, P])
        bounds = sb("bounds", [1, NSUP, 2], I32)
        bounds_in = sem("bounds_in")
        sp_passed, dve_passed, pe_passed, pool_passed = sem("sp_passed"), sem("dve_passed"), sem("pe_passed"), sem("pool_passed")
        act_passed = sem("act_passed")

        w1h = sb("w1h", [P, NX * KD, HID], F32R)
        w1l = sb("w1l", [P, NX * KD, HID], F32R)
        h32 = sb("h32", [P, 2, HID])

        with ExitStack() as edge_ctx:
            node_id = sb("node_id", [P, TILES + 1], F32, edge_ctx)
            col_id = sb("col_id", [P, P], F32, edge_ctx)
            node_parts = sb("node_parts", [P, TILES, PARTS * 2 * HEADS], BF16, edge_ctx)
            block_base = sb("block_base", [P, TILES + 1], F32, edge_ctx)
            dst_f = sb("dst_f", [P, NSUP * ET], F32, edge_ctx)
            node_tab = sb("node_tab", [P, TILES, 2 * HEADS], F32, edge_ctx)
            left = sb("left", [P, TILES, 2 * HEADS], F32, edge_ctx)
            gmax_all = sb("gmax_all", [P, 2, HEADS], F32, edge_ctx)
            shift_z = sb("shift_z", [P, TILES, HEADS], F32, edge_ctx)
            is_wide = sb("is_wide", [P, 1], I32, edge_ctx)

            def load_bounds(engine, regs, s):
                engine.load(regs, bounds[0:1, bass.ds(s, 1), :] if not isinstance(s, int) else bounds[0:1, s, :])

            def block_range(engine, regs):
                return engine.snap(regs[0], min_val=0, max_val=TILES - 1), engine.snap(regs[1], min_val=1, max_val=TILES)

            def make_node_parts(largest):
                dve = nc.vector
                dve.tensor_tensor(shift_z[:], node_tab[:, :, 0:HEADS], largest, ALU.add)
                dve.drain()
                dve.scalar_tensor_tensor(out=node_tab[:, :, HEADS:2 * HEADS], in0=shift_z[:], scalar=NEG_SLOPE,
                                         in1=shift_z[:], op0=ALU.mult, op1=ALU.max)
                dve.drain()
                part = [node_parts[:, :, k * 2 * HEADS:(k + 1) * 2 * HEADS] for k in range(PARTS)]
                dve.tensor_copy(part[0], node_tab[:])
                dve.drain()
                dve.tensor_tensor(left[:], node_tab[:], part[0], ALU.subtract)
                dve.drain()
                dve.tensor_copy(part[1], left[:])
                dve.drain()
                dve.tensor_tensor(part[2], left[:], part[1], ALU.subtract)

            with ExitStack() as c:
                xs = sb("xs", [P, TILES, D], F32, c)
                hs = sb("hs", [P, 2 * CH, ROW], F32, c)
                a_tab = sb("a_tab", [P, TILES, 2 * HEADS], F32, c)
                xn = sb("xn", [P, CH, D], F32, c)
                xTh = sb("xTh", [P, CH, D], F32R, c)
                xTl = sb("xTl", [P, CH, D], F32R, c)
                stats = sb("stats", [P, CH, 6], F32, c)
                chunk_stats = sb("chunk_stats", [P, CH, 2], F32, c)
                meanvar = sb("meanvar", [P, TILES, 2], F32, c)
                roots = sb("roots", [P, 3, TILES], F32, c)
                root_i = sb("root_i", [P, TILES], I32, c)
                rstd = sb("rstd", [P, TILES], F32, c)
                nmr = sb("nmr", [P, TILES], F32, c)
                w_aug = sb("w_aug", [P, KD, D + 2 * HEADS], F32, c)
                w_high = sb("w_high", [P, KD, D + 2 * HEADS], F32R, c)
                w_low = sb("w_low", [P, KD, D + 2 * HEADS], F32R, c)
                w_dst = sb("w_dst", [P, KD, D], F32, c)
                att_b = sb("att_b", [P, 2, D], F32, c)
                prod = sb("prod", [P, KD, D], F32, c)
                dst_i = sb("dst_i", [P, NSUP * ET], I32, c)
                rows16 = sb("rows16", [NSUP, SUP], I16, c)
                gmax = sb("gmax", [P, 2, HEADS], F32, c)
                spread = sb("spread", [P, 1 + HEADS], F32, c)
                rows = sb("rows", [NSUP, SUP], I32, c)
                lohi = sb("lohi", [NSUP, 2], F32, c)
                lohi_i = sb("lohi_i", [NSUP, 2], I32, c)
                node_id_i = sb("node_id_i", [P, TILES + 1], I32, c)
                col_id_i = sb("col_id_i", [P, P], I32, c)
                ps_T = ps("ps_T", [P, TB, 512], c)
                ps_h = ps("ps_h", [P, HB, 512], c)

                dst_in, rows16_ready, dst16_out = sem("dst_in"), sem("rows16_ready"), sem("dst16_out")
                x_in = [sem(f"x_in{u}") for u in range(2)]
                w_in, rows_in, table_out = sem("w_in"), sem("rows_in"), sem("table_out")
                consts = sem("consts")
                rstd_ready, xh_ready = sem("rstd_ready"), sem("xh_ready")
                w_ready, xn_ready, xT_done, xT_ready = sem("w_ready"), sem("xn_ready"), sem("xT_done"), sem("xT_ready")
                h_done, h_out, gmax_ready, gmax_done = sem("h_done"), sem("h_out"), sem("gmax_ready"), sem("gmax_done")
                lohi_ready = sem("lohi_ready")

                block = c.enter_context(nc.Block())

                def chunk_pairs(engine, run):
                    with engine.Fori(0, CHUNKS // 2) as i:
                        for u in range(2):
                            run(i * 2 + u, u, i)
                    for g in range(CHUNKS // 2 * 2, CHUNKS):
                        run(g, 0, g // 2)

                @block.sync
                def _(sp):
                    def load_x(g, u, i):
                        hold(sp, x_in[u], i * 16 + 16, sp_passed)
                        sp.dma_start(xs[:, bass.ds(g * CH, CH), :], x_tiles[:, bass.ds(g * CH, CH), :]).then_inc(x_in[u], 16)

                    for u in range(2):
                        sp.sem_inc(x_in[u], 16)
                    chunk_pairs(sp, load_x)
                    sp.dma_start(dst_i[:], dst_part).then_inc(dst_in, 16)
                    sp.wait_ge(rows16_ready, 1)
                    sp.dma_start(dst16, rows16[:]).then_inc(dst16_out, 16)
                    sp.wait_ge(dst16_out, 16)
                    hold(sp, lohi_ready, 1, sp_passed)
                    sp.dma_start(bounds_dram, lohi_i[:]).then_inc(bounds_in, 16)
                    hold(sp, bounds_in, 16, sp_passed)
                    sp.dma_start(bounds[:], bounds_dram[None, :, :]).then_inc(bounds_in, 16)
                    hold(sp, bounds_in, 32, sp_passed)
                    with sp.Fori(0, CHUNKS) as g:
                        hold(sp, h_out, g * CH + CH + 3, sp_passed)
                        sp.dma_start(table_tiles[:, bass.ds(g * CH, CH), :], hs[:, bass.ds((g % 2) * CH, CH), :]).then_inc(table_out, 16)
                        hold(sp, table_out, g * 16 + 48, sp_passed)

                @block.scalar
                def _(act):
                    act.dma_start(rows[:], dst_row).then_inc(rows_in, 16)
                    act.dma_start(w_aug[:, :, 0:D], W_src.rearrange("(k p) n -> p k n", p=P)).then_inc(w_in, 16)
                    act.dma_start(w_dst[:], W_dst.rearrange("(k p) n -> p k n", p=P)).then_inc(w_in, 16)
                    act.dma_start(att_b[:, 0, :], att_src.partition_broadcast(P)).then_inc(w_in, 16)
                    act.dma_start(att_b[:, 1, :], att_dst.partition_broadcast(P)).then_inc(w_in, 16)

                    def normalise(g, j):
                        t = g * CH + j
                        act.wait_ge(xT_done, t + 1)
                        nc.scalar.activation(xn[:, j, :], xs[:, bass.ds(t, 1), :], ACT.Identity,
                                             bias=nmr[:, bass.ds(t, 1)], scale=rstd[:, bass.ds(t, 1)]).then_inc(xn_ready, 1)

                    act.wait_ge(rstd_ready, 1)
                    with act.Fori(0, CHUNKS) as g:
                        normalise(g, 0)
                        normalise(g, 1)
                        for j in range(CH):
                            t = g * CH + j
                            if j + 2 < CH:
                                normalise(g, j + 2)
                            act.wait_ge(h_done, t + 1)
                            act.wait_ge(xT_done, t + CH + 1)
                            nc.scalar.copy(xTh[:, j, :], ps_T[:, j % TB, 0:D]).then_inc(xh_ready, 1)

                @block.gpsimd
                def _(pool):
                    nc.gpsimd.memset(ident[:], 0.0)
                    nc.gpsimd.iota(node_id_i[:], pattern=[[P, TILES + 1]], base=0, channel_multiplier=1)
                    nc.gpsimd.iota(col_id_i[:], pattern=[[1, P]], base=0, channel_multiplier=0)
                    pool.drain()
                    nc.gpsimd.tensor_copy(node_id[:], node_id_i[:])
                    nc.gpsimd.tensor_copy(col_id[:], col_id_i[:])
                    nc.gpsimd.affine_select(out=ident[:], in_=ident[:], compare_op=ALU.not_equal, fill=1.0, base=0,
                                            pattern=[[-1, P]], channel_multiplier=1)
                    pool.drain()
                    nc.gpsimd.memset(gmax_all[:], 0.0).then_inc(consts, 1)
                    pool.wait_ge(consts, 1)
                    pool.wait_ge(gmax_ready, 1)
                    nc.gpsimd.partition_all_reduce(gmax_all[:], gmax[:], P, bass.bass_isa.ReduceOp.max).then_inc(gmax_done, 1)

                @block.vector
                def _(dve):
                    dve.sem_inc(h_out, 3)
                    dve.sem_inc(table_out, 32)

                    dve.wait_ge(rows_in, 16)
                    nc.vector.tensor_copy(rows16[:], rows[:]).then_inc(rows16_ready, 1)
                    nc.vector.tensor_reduce(lohi[:, 0:1], rows[:], AX.X, ALU.min)
                    nc.vector.tensor_reduce(lohi[:, 1:2], rows[:], AX.X, ALU.max)
                    dve.drain()
                    nc.vector.tensor_copy(lohi_i[:], lohi[:])
                    dve.drain()
                    nc.vector.tensor_scalar(lohi_i[:], lohi_i[:], 7, None, ALU.arith_shift_right)
                    dve.drain()
                    nc.vector.tensor_scalar(lohi_i[:, 1:2], lohi_i[:, 1:2], 1, None, ALU.add).then_inc(lohi_ready, 1)
                    dve.wait_ge(w_in, 64)
                    for side, w in ((0, w_aug[:, :, 0:D]), (1, w_dst[:])):
                        nc.vector.tensor_tensor(prod[:], w, att_b[:, side, :].unsqueeze(1).to_broadcast([P, KD, D]), ALU.mult)
                        dve.drain()
                        lo = D + side * HEADS
                        nc.vector.tensor_reduce(w_aug[:, :, lo:lo + HEADS], prod[:].rearrange("p k (h c) -> p k h c", h=HEADS),
                                                AX.X, ALU.add)
                        dve.drain()
                    nc.vector.tensor_copy(w_high[:], w_aug[:])
                    dve.drain()
                    nc.vector.tensor_tensor(w_low[:], w_aug[:], w_high[:].bitcast(F32), ALU.subtract).then_inc(w_ready, 1)

                    def statistics(g, u, i):
                        dve.wait_ge(x_in[u], i * 16 + 32)
                        for j in range(CH):
                            nc.vector.bn_stats(stats[:, j, :], xs[:, bass.ds(g * CH + j, 1), :])
                        dve.drain()
                        for j in range(CH):
                            nc.vector.bn_aggr(chunk_stats[:, j, :], stats[:, j, :])
                        dve.drain()
                        nc.vector.tensor_copy(meanvar[:, bass.ds(g * CH, CH), :], chunk_stats[:])

                    chunk_pairs(dve, statistics)
                    dve.drain()
                    inverse_root(nc, meanvar[:, :, 1], roots, root_i, rstd[:])
                    nc.vector.scalar_tensor_tensor(out=nmr[:], in0=meanvar[:, :, 0], scalar=-1.0, in1=rstd[:],
                                                   op0=ALU.mult, op1=ALU.mult).then_inc(rstd_ready, 1)
                    dve.wait_ge(dst_in, 16)
                    nc.vector.tensor_copy(dst_f[:], dst_i[:])
                    dve.wait_ge(consts, 1)
                    nc.vector.tensor_scalar(block_base[:], node_id[:], node_id[:, 0:1], None, ALU.subtract)
                    with dve.Fori(0, CHUNKS) as g:
                        def out_of_bank(j):
                            t = g * CH + j
                            dve.wait_ge(h_done, t + CH + 1)
                            if j == 0:
                                hold(dve, table_out, g * 16 + 16, dve_passed)
                            nc.vector.tensor_copy(hs[:, bass.ds((g % 2) * CH + j, 1), :], ps_h[:, j % HB, 0:ROW].unsqueeze(1))
                            nc.vector.tensor_copy(a_tab[:, bass.ds(t, 1), :], ps_h[:, j % HB, D:ROW + HEADS].unsqueeze(1)).then_inc(h_out, 1)

                        for j in range(CH):
                            dve.wait_ge(xh_ready, g * CH + j + 1)
                            nc.vector.tensor_tensor(xTl[:, j, :], ps_T[:, j % TB, 0:D], xTh[:, j, :].bitcast(F32),
                                                    ALU.subtract).then_inc(xT_ready, 1)
                            if j > 0:
                                out_of_bank(j - 1)
                        out_of_bank(CH - 1)
                    dve.drain()
                    nc.vector.tensor_copy(node_tab[:, :, 0:HEADS], a_tab[:, :, HEADS:2 * HEADS])
                    dve.drain()
                    a_src = a_tab[:, :, 0:HEADS].rearrange("p t h -> p h t")
                    nc.vector.tensor_reduce(gmax[:, 0, :], a_src, AX.X, ALU.max)
                    nc.vector.tensor_reduce(gmax[:, 1, :], a_src, AX.X, ALU.min)
                    dve.drain()
                    nc.vector.tensor_scalar(gmax[:, 1, :], gmax[:, 1, :], -1.0, None, ALU.mult).then_inc(gmax_ready, 1)
                    dve.wait_ge(gmax_done, 1)
                    nc.vector.tensor_tensor(spread[:, 1:1 + HEADS], gmax_all[:, 0, :], gmax_all[:, 1, :], ALU.add)
                    dve.drain()
                    nc.vector.tensor_reduce(spread[:, 0:1], spread[:, 1:1 + HEADS], AX.X, ALU.max)
                    dve.drain()
                    nc.vector.tensor_scalar(is_wide[:], spread[:, 0:1], MAX_SPREAD, None, ALU.is_gt)
                    make_node_parts(gmax_all[:, 0, :].unsqueeze(1).to_broadcast([P, TILES, HEADS]))

                @block.tensor
                def _(pe):
                    pe.sem_inc(xT_done, CH)
                    pe.sem_inc(h_done, CH)
                    pe.wait_ge(consts, 1)
                    pe.wait_ge(w_ready, 1)

                    def transpose(g, j):
                        pe.wait_ge(xn_ready, g * CH + j + 1)
                        for k in range(KD):
                            i = nc.tensor.transpose(ps_T[:, j % TB, k * P:(k + 1) * P], xn[:, j, k * P:(k + 1) * P], ident[:])
                        i.then_inc(xT_done, 1)

                    with pe.Fori(0, CHUNKS) as g:
                        transpose(g, 0)
                        transpose(g, 1)
                        for j in range(CH):
                            t = g * CH + j
                            if j + 2 < CH:
                                transpose(g, j + 2)
                            pe.wait_ge(h_out, t + 1)
                            pe.wait_ge(xT_ready, t + 1)
                            for k in range(KD):
                                high, low = (part[:, j, k * P:(k + 1) * P] for part in (xTh, xTl))
                                for n, (a, w) in enumerate(((high, w_high), (high, w_low), (low, w_high))):
                                    i = nc.tensor.matmul(ps_h[:, j % HB, 0:ROW + HEADS], a, w[:, k, :],
                                                         start=(k + n == 0), stop=(k == KD - 1 and n == 2))
                            i.then_inc(h_done, 1)

            with ExitStack() as c:
                rows_g = sb("rows_g", [P, ET, ROW], F32, c)
                idx_g = sb("idx_g", [P, ET], I32, c)
                row_g = sb("row_g", [P, SUP], I16, c)
                diag = sb("diag", [P, HEADS, P], F32, c)
                ones = sb("ones", [P, P], F32, c)
                a_edge = sb("a_edge", [P, HEADS, ET, P], F32, c)
                masked = sb("masked", [P, HEADS, ET, P], F32, c)
                other = sb("other", [P, SUP], F32, c)
                largest = sb("largest", [P, TILES, HEADS], F32, c)
                new = sb("new", [P, 1, HEADS], F32, c)
                ps_a = ps("ps_a", [P, HEADS, P], c)
                idx_got, row_got, rows_got, rows_used = sem("idx_got"), sem("row_got"), sem("rows_got"), sem("rows_used")
                diag_ready, a_done = sem("diag_ready"), sem("a_done")
                block = c.enter_context(nc.Block())

                def where_wide(engine):
                    flag = engine.alloc_register("is_wide")
                    engine.load(flag, is_wide[0:1, 0:1])
                    return engine.If(engine.snap(flag, min_val=0, max_val=1) > 0)

                @block.gpsimd
                def _(pool):
                    with where_wide(pool):
                        with pool.Fori(0, NSUP) as s:
                            hold(pool, rows_used, s + 1, pool_passed)
                            pool.dma_start(idx_g[:], src_idx[bass.ds(s, 1)].rearrange("a p r -> (a p) r")).then_inc(idx_got, 16)
                            pool.dma_start(row_g[:], dst16[bass.ds(s, 1), :].partition_broadcast(P)).then_inc(row_got, 16)
                            hold(pool, idx_got, s * 16 + 16, pool_passed)
                            for r in range(ET):
                                nc.gpsimd.indirect_dma_start(
                                    out=rows_g[:, r, :], out_offset=None, in_=table,
                                    in_offset=bass.IndirectOffsetOnAxis(ap=idx_g[:, r:r + 1], axis=0)
                                ).then_inc(rows_got, 16)

                @block.vector
                def _(dve):
                    with where_wide(dve):
                        dve.sem_inc(rows_used, 1)
                        nc.vector.memset(ones[:], 1.0)
                        nc.vector.memset(largest[:], LOWEST)
                        dve.drain()
                        regs = [dve.alloc_register(f"blocks{k}") for k in range(2)]
                        with dve.Fori(0, NSUP) as s:
                            hold(dve, rows_got, s * (16 * ET) + 16 * ET, dve_passed)
                            for r in range(ET):
                                for h in range(HEADS):
                                    i = nc.vector.tensor_scalar(diag[:, h, :], ident[:], rows_g[:, r, D + h:D + h + 1], None, ALU.mult)
                                i.then_inc(diag_ready, 1)
                                dve.wait_ge(a_done, s * ET + r + 1)
                                nc.vector.tensor_copy(a_edge[:, :, r, :], ps_a[:])
                            hold(dve, row_got, s * 16 + 16, dve_passed)
                            load_bounds(dve, regs, s)
                            lo, end = block_range(dve, regs)
                            with dve.Fori(lo, end) as b:
                                nc.vector.tensor_scalar(other[:], row_g[:], node_id[:, bass.ds(b, 1)], LOWEST, ALU.not_equal, ALU.mult)
                                dve.drain()
                                nc.vector.tensor_tensor(masked[:], a_edge[:], other[:].rearrange("p (r e) -> p r e", e=P).unsqueeze(1)
                                                        .to_broadcast([P, HEADS, ET, P]), ALU.add)
                                dve.drain()
                                nc.vector.tensor_reduce(new[:, 0, :], masked[:].rearrange("p h r e -> p h (r e)"), AX.X, ALU.max)
                                dve.drain()
                                best = largest[:, bass.ds(b, 1), :]
                                nc.vector.tensor_tensor(best, best, new[:], ALU.max)
                                dve.drain()
                            dve.drain().then_inc(rows_used, 1)
                        nc.vector.tensor_scalar(gmax_all[:, 1, :], gmax_all[:, 1, :], -1.0, None, ALU.mult)
                        dve.drain()
                        nc.vector.tensor_tensor(largest[:], largest[:], gmax_all[:, 1, :].unsqueeze(1).to_broadcast([P, TILES, HEADS]), ALU.max)
                        dve.drain()
                        make_node_parts(largest[:])

                @block.tensor
                def _(pe):
                    with where_wide(pe):
                        with pe.Fori(0, NSUP * ET) as n:
                            pe.wait_ge(diag_ready, n + 1)
                            nc.tensor.matmul(ps_a[:], ones[:], diag[:], start=True, stop=True).then_inc(a_done, 1)

            with ExitStack() as c:
                acc = sb("acc", [P, TILES + 1, ROW], F32, c)
                msg = sb("msg", [P, SLOTS, ET, ROW], F32, c)
                idx = sb("idx", [P, SLOTS, ET], I32, c)
                row_b = sb("row_b", [P, 2, SUP], I16, c)
                sel_n = sb("sel_n", [P, 2, 2, 2, SUP // 2], BF16, c)
                sel_e = sb("sel_e", [P, 3, 2, ET // 2, P], F32, c)
                edge_tab = sb("edge_tab", [P, ET, 2 * HEADS], F32, c)
                score = sb("score", [P, 2, ET, HEADS], F32, c)
                zeros = sb("zeros", [1, PARTS * ET * 2 * HEADS], BF16, c)
                ps_tab = ps("ps_tab", [P, 2, 512], c)
                ps_agg = ps("ps_agg", [P, 3, 512], c)
                idx_in = [sem(f"idx_in{u}") for u in range(SLOTS)]
                gathered = [sem(f"gathered{u}") for u in range(SLOTS)]
                row_in = [sem(f"row_in{u}") for u in range(2)]
                row_used, zeros_ready = sem("row_used"), sem("zeros_ready")
                seln_ready = [sem(f"seln_ready{h}") for h in range(2)]
                tab_done, tab_out = sem("tab_done"), sem("tab_out")
                score_ready, p_ready, msg_ready, msg_used = sem("score_ready"), sem("p_ready"), sem("msg_ready"), sem("msg_used")
                sele_ready = [sem(f"sele_ready{h}") for h in range(2)]
                seln_used, agg_done = sem("seln_used"), sem("agg_done")
                w1_in, w1_high, w1_used = sem("w1_in"), sem("w1_high"), sem("w1_used")
                acc_ready, sums_out = sem("acc_ready"), sem("sums_out")
                block = c.enter_context(nc.Block())
                HALF = ET // 2
                TURNS = (NSUP - 2) // SLOTS
                assert TURNS == NX * KD
                W1_rows = W1.rearrange("e (k p) n -> p (e k) n", p=P)

                def steps(engine, step):
                    with engine.Fori(0, TURNS) as i:
                        for u in range(SLOTS):
                            step(i * SLOTS + u, u, i, 2)
                    for u in range(2):
                        step(TURNS * SLOTS + u, u, TURNS, 1 - u)

                def ahead(s, u, i, k):
                    return s + k, (u + k) % SLOTS, i + (u + k) // SLOTS

                @block.sync
                def _(sp):
                    for u in range(SLOTS):
                        sp.dma_start(idx[:, u, :], src_idx[u]).then_inc(idx_in[u], 16)
                    for u in range(2):
                        sp.dma_start(row_b[:, u, :], dst16[u:u + 1, :].partition_broadcast(P)).then_inc(row_in[u], 16)
                    with sp.Fori(0, (NSUP - SLOTS - 2) // SLOTS) as i:
                        for u in range(SLOTS):
                            s = i * SLOTS + u
                            hold(sp, row_used, s + 1, sp_passed)
                            sp.dma_start(row_b[:, u % 2, :], dst16[bass.ds(s + 2, 1), :].partition_broadcast(P)).then_inc(row_in[u % 2], 16)
                            hold(sp, gathered[u], i * (16 * ET) + 16 * ET, sp_passed)
                            sp.dma_start(idx[:, u, :], src_idx[bass.ds(s + SLOTS, 1)].rearrange("a p r -> (a p) r")).then_inc(idx_in[u], 16)
                    for s in range(NSUP - SLOTS - 2, NSUP - 2):
                        sp.wait_ge(row_used, s + 1)
                        sp.dma_start(row_b[:, s % 2, :], dst16[s + 2:s + 3, :].partition_broadcast(P)).then_inc(row_in[s % 2], 16)
                        if s + SLOTS < NSUP:
                            sp.wait_ge(gathered[s % SLOTS], (s // SLOTS + 1) * 16 * ET)
                            sp.dma_start(idx[:, s % SLOTS, :], src_idx[s + SLOTS]).then_inc(idx_in[s % SLOTS], 16)
                    sp.wait_ge(acc_ready, 1)
                    sp.dma_start(sums_tiles, acc[:, 0:TILES, :]).then_inc(sums_out, 16)
                    sp.wait_ge(sums_out, 16)

                @block.gpsimd
                def _(pool):
                    def step(s, u, i, behind):
                        pool.wait_ge(idx_in[u], i * 16 + 16)
                        hold(pool, msg_used, s + 1, pool_passed)
                        for r in range(ET):
                            nc.gpsimd.indirect_dma_start(
                                out=msg[:, u, r, :], out_offset=None, in_=table,
                                in_offset=bass.IndirectOffsetOnAxis(ap=idx[:, u, r:r + 1], axis=0)
                            ).then_inc(gathered[u], 16)
                    steps(pool, step)

                @block.scalar
                def _(act):
                    def weigh(s, u):
                        act.wait_ge(score_ready, s + 1)
                        nc.scalar.activation(msg[:, u, :, D:ROW], score[:, u % 2, :, :], ACT.Exp).then_inc(p_ready, 1)

                    def step(s, u, i, behind):
                        if behind == 2 and u == 0:
                            hold(act, w1_used, i + 1, act_passed)
                            act.dma_start(h32[:, 0:1, :], W1_rows[:, bass.ds(i, 1), :]).then_inc(w1_in, 16)
                        if behind == 2 and u == 2:
                            act.wait_ge(w1_in, i * 16 + 16)
                            nc.scalar.copy(w1h[:, bass.ds(i, 1), :], h32[:, 0:1, :]).then_inc(w1_high, 1)
                        if behind == 2:
                            weigh(*ahead(s, u, i, 2)[:2])
                    weigh(0, 0)
                    weigh(1, 1)
                    steps(act, step)

                @block.vector
                def _(dve):
                    dve.sem_inc(msg_used, SLOTS - 1)
                    nc.vector.memset(zeros[:], 0.0)
                    nc.vector.memset(ps_agg[:], 0.0)
                    dve.sem_inc(w1_used, 1)
                    dve.drain().then_inc(zeros_ready, 1)
                    npair, added, b_prev, bank_prev = (dve.alloc_register(n) for n in ("npair", "added", "b_prev", "bank_prev"))
                    now, nxt, then = ([dve.alloc_register(f"{n}{k}") for k in range(2)] for n in ("now", "next", "then"))
                    dve.reg_mov(npair, 0)
                    dve.reg_mov(added, 0)
                    dve.reg_mov(b_prev, TILES)
                    dve.reg_mov(bank_prev, 1)

                    def select_nodes(s, u, i, regs):
                        lo, end = block_range(dve, regs)

                        def select(b, slot):
                            for h in range(2):
                                nc.vector.tensor_scalar(sel_n[:, u % 2, slot, h, :], row_b[:, u % 2, h * (SUP // 2):(h + 1) * (SUP // 2)],
                                                        node_id[:, bass.ds(b, 1)], None, ALU.is_equal).then_inc(seln_ready[h], 1)
                            dve.reg_add(npair, npair, 1)

                        hold(dve, row_in[u % 2], (s // 2 if isinstance(s, int) else i * (SLOTS // 2) + u // 2) * 16 + 16, dve_passed)
                        select(lo, 0)
                        with dve.If(end > lo + 1):
                            select(lo + 1, 1)
                        with dve.If(end > lo + 2):
                            with dve.Fori(lo + 2, end) as b:
                                hold(dve, seln_used, dve.snap(npair), dve_passed)
                                select(b, 1)
                        dve.drain().then_inc(row_used, 1)

                    def scores(s, u, i):
                        sc = score[:, u % 2, :, :]
                        dve.wait_ge(tab_done, s + 1)
                        nc.vector.tensor_reduce(edge_tab[:], ps_tab[:, u % 2, 0:PARTS * ET * 2 * HEADS].rearrange(
                            "p (r k c) -> p r c k", r=ET, k=PARTS), AX.X, ALU.add).then_inc(tab_out, 1)
                        dve.drain()
                        dve.wait_ge(gathered[u], i * (16 * ET) + 16 * ET)
                        nc.vector.tensor_tensor(sc, msg[:, u, :, D:ROW], edge_tab[:, :, 0:HEADS], ALU.add)
                        dve.drain()
                        nc.vector.scalar_tensor_tensor(out=sc, in0=sc, scalar=NEG_SLOPE, in1=sc, op0=ALU.mult, op1=ALU.max)
                        dve.drain()
                        nc.vector.tensor_tensor(sc, sc, edge_tab[:, :, HEADS:2 * HEADS], ALU.subtract).then_inc(score_ready, 1)

                    def weigh(s, u):
                        dve.wait_ge(p_ready, s + 1)
                        h4 = msg[:, u, :, 0:D].rearrange("p r (h c) -> p r h c", h=HEADS)
                        nc.vector.tensor_tensor(h4, h4, msg[:, u, :, D:ROW].unsqueeze(3).to_broadcast([P, ET, HEADS, HC]),
                                                ALU.mult).then_inc(msg_ready, 1)

                    def add_last():
                        dve.wait_ge(agg_done, dve.snap(added) + 1)
                        b = dve.snap(b_prev, min_val=0, max_val=TILES)
                        bank = dve.snap(bank_prev, min_val=0, max_val=2)
                        return nc.vector.tensor_tensor(acc[:, bass.ds(b, 1), :], acc[:, bass.ds(b, 1), :],
                                                       ps_agg[:, bass.ds(bank, 1), 0:ROW], ALU.add)

                    def pending(b, bank):
                        dve.reg_add(added, added, 1)
                        dve.reg_mov(b_prev, b)
                        dve.reg_mov(bank_prev, bank)

                    def step(s, u, i, behind):
                        if behind == 2:
                            load_bounds(dve, then, s + 2)
                            select_nodes(*ahead(s, u, i, 2), then)

                        def select(b, slot):
                            for h in range(2):
                                dst = dst_f[:, bass.ds(s * ET + h * HALF, HALF)]
                                nc.vector.scalar_tensor_tensor(
                                    out=sel_e[:, slot, h, :, :], in0=col_id[:].unsqueeze(1).to_broadcast([P, HALF, P]),
                                    scalar=block_base[:, bass.ds(b, 1)], in1=dst.unsqueeze(2).to_broadcast([P, HALF, P]),
                                    op0=ALU.add, op1=ALU.is_equal).then_inc(sele_ready[h], 1)

                        lo, end = block_range(dve, now)
                        select(lo, u % 2)
                        add_last().then_inc(msg_used, 1)
                        pending(lo, u % 2)
                        with dve.If(end > lo + 1):
                            select(lo + 1, 2)
                        if behind >= 1:
                            weigh(*ahead(s, u, i, 1)[:2])
                        if behind == 2:
                            scores(*ahead(s, u, i, 2))
                        if behind == 2 and u == 3:
                            dve.wait_ge(w1_high, i + 1)
                            nc.vector.tensor_tensor(w1l[:, bass.ds(i, 1), :], h32[:, 0:1, :],
                                                    w1h[:, bass.ds(i, 1), :].bitcast(F32), ALU.subtract).then_inc(w1_used, 1)
                        with dve.If(end > lo + 1):
                            dve.drain()
                            add_last()
                            pending(lo + 1, 2)
                        with dve.If(end > lo + 2):
                            with dve.Fori(lo + 2, end) as b:
                                dve.drain()
                                add_last()
                                select(b, 2)
                                pending(b, 2)
                        for k in range(2):
                            dve.reg_mov(now[k], nxt[k])
                            dve.reg_mov(nxt[k], then[k])

                    load_bounds(dve, now, 0)
                    load_bounds(dve, nxt, 1)
                    select_nodes(0, 0, 0, now)
                    select_nodes(1, 1, 0, nxt)
                    nc.vector.memset(acc[:], 0.0)
                    scores(0, 0, 0)
                    dve.drain()
                    weigh(0, 0)
                    scores(1, 1, 0)
                    steps(dve, step)
                    dve.drain()
                    add_last().then_inc(acc_ready, 1)

                @block.tensor
                def _(pe):
                    pe.sem_inc(agg_done, 1)
                    pe.sem_inc(tab_out, 2)
                    pe.wait_ge(zeros_ready, 1)
                    npair, epair = pe.alloc_register("npair"), pe.alloc_register("epair")
                    now, nxt, then = ([pe.alloc_register(f"{n}{k}") for k in range(2)] for n in ("now", "next", "then"))
                    pe.reg_mov(npair, 0)
                    pe.reg_mov(epair, 0)
                    W = PARTS * 2 * HEADS

                    def tables(s, u, regs):
                        lo, end = block_range(pe, regs)
                        pe.wait_ge(tab_out, s + 1)
                        bank = ps_tab[:, u % 2, 0:ET * W]
                        nc.tensor.matmul(bank, zeros[:, 0:P], zeros[:], start=True, stop=False)

                        def look_up(b, slot):
                            pe.reg_add(npair, npair, 1)
                            n = pe.snap(npair)
                            for h in range(2):
                                pe.wait_ge(seln_ready[h], n)
                                for r in range(HALF):
                                    at = (h * HALF + r) * W
                                    m = nc.tensor.matmul(bank[:, at:at + W], sel_n[:, u % 2, slot, h, r * P:(r + 1) * P],
                                                         node_parts[:, bass.ds(b, 1), :], start=False, stop=False)
                            m.then_inc(seln_used, 1)

                        look_up(lo, 0)
                        with pe.If(end > lo + 1):
                            with pe.Fori(lo + 1, end) as b:
                                look_up(b, 1)
                        nc.tensor.matmul(bank, zeros[:, 0:P], zeros[:], start=False, stop=True).then_inc(tab_done, 1)

                    def step(s, u, i, behind):
                        if behind == 2:
                            load_bounds(pe, then, s + 2)
                            tables(*ahead(s, u, i, 2)[:2], then)
                        hold(pe, msg_ready, s + 1, pe_passed)
                        lo, end = block_range(pe, now)

                        def sum_up(slot):
                            pe.reg_add(epair, epair, 1)
                            n = pe.snap(epair)
                            for h in range(2):
                                pe.wait_ge(sele_ready[h], n)
                                for r in range(HALF):
                                    m = nc.tensor.matmul(ps_agg[:, slot, 0:ROW], sel_e[:, slot, h, r, :], msg[:, u, h * HALF + r, :],
                                                         start=(h + r == 0), stop=(h * HALF + r == ET - 1))
                            m.then_inc(agg_done, 1)

                        sum_up(u % 2)
                        with pe.If(end > lo + 1):
                            with pe.Fori(lo + 1, end) as b:
                                sum_up(2)
                        for k in range(2):
                            pe.reg_mov(now[k], nxt[k])
                            pe.reg_mov(nxt[k], then[k])

                    load_bounds(pe, now, 0)
                    load_bounds(pe, nxt, 1)
                    tables(0, 0, now)
                    tables(1, 1, nxt)
                    steps(pe, step)

        with ExitStack() as c:
            w2h = sb("w2h", [P, NX * KH, D], F32R, c)
            w2l = sb("w2l", [P, NX * KH, D], F32R, c)
            wgh = sb("wgh", [P, KD, NX], F32R, c)
            wgl = sb("wgl", [P, KD, NX], F32R, c)
            wg = sb("wg", [P, KD, NX], F32, c)
            gate_b = sb("gate_b", [P, 2, NX], F32, c)
            b1_rows = sb("b1_rows", [NX * KH, P], F32, c)
            b1T = sb("b1T", [P, NX * KH], F32, c)
            b2_sb = sb("b2_sb", [NX, D], F32, c)
            vec = sb("vec", [P, 4, D], F32, c)
            ramp_i = sb("ramp_i", [P, GT, NX], I32, c)
            ramp = sb("ramp", [P, GT, NX], F32, c)
            sums = sb("sums", [P, GT, ROW], F32, c)
            tmp = sb("tmp", [P, GT, D], F32, c)
            rden = sb("rden", [P, GT, HEADS], F32, c)
            y = sb("y", [P, 2 * GT, D], F32, c)
            xTh = sb("xTh3", [P, 2 * KD, GT * P], F32R, c)
            xTl = sb("xTl3", [P, 2 * KD, GT * P], F32R, c)
            hh = sb("hh", [P, 2 * KH, GT * P], F32R, c)
            hl = sb("hl", [P, 2 * KH, GT * P], F32R, c)
            stats = sb("stats3", [P, GT, 6], F32, c)
            meanvar = sb("meanvar3", [P, GT, 2], F32, c)
            rstd = sb("rstd3", [P, GT], F32, c)
            roots = sb("roots3", [P, 3, GT], F32, c)
            root_i = sb("root_i3", [P, GT], I32, c)
            eight_rows = sb("eight_rows", [NX, GT * P], F32, c)
            logit = sb("logit", [P, GT, NX], F32, c)
            work = sb("work", [P, GT, NX], F32, c)
            pick = sb("pick", [P, 2, GT, NX], F32, c)
            top = sb("top", [P, 2, GT], F32, c)
            first = sb("first", [P, GT], F32, c)
            gap = sb("gap", [P, GT], F32, c)
            wts = sb("wts", [P, 2, GT], F32, c)
            comb_new = sb("comb_new", [P, GT, NX], F32, c)
            comb = sb("comb", [P, 2 * GT, NX], F32, c)
            ps_h = ps("ps_h3", [P, KH, 512], c)
            ps_y = ps("ps_y3", [P, YB, 512], c)
            ps_p = ps("ps_p3", [P, 2, 512], c)

            RAW = 4
            small_in, raw_in, raw_used, raw_hi = sem("small_in"), [sem(f"raw_in{u}") for u in range(RAW)], sem("raw_used"), sem("raw_hi")
            ramp_ready, b1T_done, b1T_ready, weights_ready = sem("ramp_ready"), sem("b1T_done"), sem("b1T_ready"), sem("weights_ready")
            sums_in, x3_in, y_out = sem("sums_in"), sem("x3_in"), sem("y_out")
            rden_ready, o_ready, affine_ready, pos_ready, x1_ready = (sem("rden_ready"), sem("o_ready"), sem("affine_ready"),
                                                                      sem("pos_ready"), sem("x1_ready"))
            norm_ready, vec_in = sem("norm_ready"), sem("vec_in")
            xT_done, xh_ready, xl_ready = sem("xT3_done"), sem("xh3_ready"), sem("xl_ready")
            logitT_done, logitT_ready, logit_done, gap_ready, e_ready = (sem("logitT_done"), sem("logitT_ready"), sem("logit_done"),
                                                                         sem("gap_ready"), sem("e_ready"))
            comb_ready, combT_done, combT_ready, b2_done, b2_added = (sem("comb_ready"), sem("combT_done"), sem("combT_ready"),
                                                                      sem("b2_done"), sem("b2_added"))
            h_done, h_out, hT_ready, y_done, y_added = sem("h3_done"), sem("h3_out"), sem("hT_ready"), sem("y3_done"), sem("y3_added")
            HU = NX * KH
            block = c.enter_context(nc.Block())

            def all_groups(engine, run):
                with engine.Fori(0, GROUPS - 1) as g:
                    run(g, GT, GT, g * (NX * GT))
                run(GROUPS - 1, GT, 1, (GROUPS - 1) * NX * GT)
                run(GROUPS, 1, 0, GROUPS * NX * GT)

            def at(tensor, g, slots, j=0, n=1):
                return tensor[:, bass.ds((g % 2) * slots + j, n), :]

            PIECES = NX * KH * D // HID
            KQ = HID // D

            def w2_loop(engine, part, run):
                turns = PIECES // RAW // 2
                with engine.Fori(part * turns, (part + 1) * turns) as i:
                    for u in range(RAW):
                        run(i * RAW + u, u, i)

            def piece(weights, q):
                return weights[:, bass.ds(q * KQ, KQ), :]

            def raw(u):
                return h32[:, u, :].rearrange("p (k n) -> p k n", n=D) if u < 2 else y[:, GT + (u - 2) * KQ:GT + (u - 1) * KQ, :]

            @block.sync
            def _(sp):
                def load_sums(tile, tiles):
                    sp.dma_start(sums[:, 0:tiles, :], sums_tiles[:, bass.ds(tile, tiles), :]).then_inc(sums_in, 16)

                def load_x(g, tiles):
                    sp.dma_start(at(y, g, GT, 0, tiles), x_tiles[:, bass.ds(g * GT, tiles), :]).then_inc(x3_in, 16)

                load_sums(0, GT)
                for k, v in enumerate((bias, ln_gamma, ln_beta, prelu_w)):
                    sp.dma_start(vec[:, k, :], v.partition_broadcast(P)).then_inc(vec_in, 16)
                load_x(0, GT)
                W2_rows = W2.rearrange("e (k p) n -> p (e k) n", p=P)

                def load_w2(q, u, i):
                    sp.wait_ge(raw_used, q + 1)
                    sp.dma_start(raw(u), W2_rows[:, bass.ds(q * KQ, KQ), :]).then_inc(raw_in[u], 16)

                w2_loop(sp, 0, load_w2)
                w2_loop(sp, 1, load_w2)
                sp.wait_ge(weights_ready, 1)

                def run(g, tiles, tiles_next, sums_before):
                    if tiles_next:
                        hold(sp, x1_ready, g + 1, sp_passed)
                        load_sums(g * GT + GT, tiles_next)
                        hold(sp, y_out, 16 * g + 16, sp_passed)
                        load_x(g + 1, tiles_next)
                    hold(sp, y_added, sums_before + NX * tiles + YB, sp_passed)
                    sp.dma_start(out_tiles[:, bass.ds(g * GT, tiles), :], at(y, g, GT, 0, tiles)).then_inc(y_out, 16)

                all_groups(sp, run)
                sp.wait_ge(y_out, 16 * (GROUPS + 1) + 16)

            @block.gpsimd
            def _(pool):
                pool.sem_inc(y_out, 16)
                nc.gpsimd.iota(ramp_i[:], pattern=[[0, GT], [1, NX]], base=-NX, channel_multiplier=0)
                pool.drain()
                nc.gpsimd.tensor_copy(ramp[:], ramp_i[:]).then_inc(ramp_ready, 1)
                pool.wait_ge(vec_in, 16 * 4)

                def prepare(g, tiles):
                    def row(k):
                        return vec[:, k, :].unsqueeze(1).to_broadcast([P, tiles, D])

                    o = sums[:, 0:tiles, 0:D]
                    pool.wait_ge(rden_ready, g + 1)
                    for j in range(tiles):
                        oj = sums[:, j, 0:D].rearrange("p (h c) -> p h c", h=HEADS)
                        nc.gpsimd.tensor_tensor(oj, oj, rden[:, j, :].unsqueeze(2).to_broadcast([P, HEADS, HC]), ALU.mult)
                    pool.drain()
                    nc.gpsimd.tensor_tensor(o, o, row(0), ALU.add).then_inc(o_ready, 1)
                    pool.wait_ge(norm_ready, 2 * g + 1)
                    nc.gpsimd.tensor_tensor(o, o, row(1), ALU.mult)
                    pool.drain()
                    nc.gpsimd.tensor_tensor(o, o, row(2), ALU.add).then_inc(affine_ready, 1)
                    yg = at(y, g, GT, 0, tiles)
                    pool.wait_ge(pos_ready, 2 * g + 1)
                    pool.wait_ge(x3_in, 16 * g + 16)
                    nc.gpsimd.tensor_tensor(yg, yg, tmp[:, 0:tiles, :], ALU.add)
                    pool.wait_ge(pos_ready, 2 * g + 2)
                    nc.gpsimd.tensor_tensor(o, o, row(3), ALU.mult)
                    pool.drain()
                    nc.gpsimd.tensor_tensor(yg, yg, o, ALU.subtract).then_inc(x1_ready, 1)

                prepare(0, GT)

                def run(g, tiles, tiles_next, sums_before):
                    if tiles_next:
                        prepare(g + 1, tiles_next)

                all_groups(pool, run)

            @block.scalar
            def _(act):
                act.dma_start(wg[:], Wg.rearrange("(k p) n -> p k n", p=P)).then_inc(small_in, 16)
                act.dma_start(gate_b[:, 0, :], bg.partition_broadcast(P)).then_inc(small_in, 16)
                act.dma_start(gate_b[:, 1, :], gbias.partition_broadcast(P)).then_inc(small_in, 16)
                act.dma_start(b1_rows[:], b1.rearrange("e (k p) -> (e k) p", p=P)).then_inc(small_in, 16)
                act.dma_start(b2_sb[:], b2).then_inc(small_in, 16)
                act.wait_ge(b1T_done, 1)
                nc.scalar.copy(b1T[:], ps_y[:, 0, 0:NX * KH]).then_inc(b1T_ready, 1)

                def halves(g, tiles):
                    act.wait_ge(affine_ready, g + 1)
                    o = sums[:, 0:tiles, 0:D]
                    nc.scalar.activation(tmp[:, 0:tiles, :], o, ACT.Relu).then_inc(pos_ready, 1)
                    nc.scalar.activation(o, o, ACT.Relu, scale=-1.0).then_inc(pos_ready, 1)

                def high_parts(g, tiles):
                    act.wait_ge(xT_done, g + 1)
                    for k in range(KD):
                        nc.scalar.copy(at(xTh, g, KD, k)[:, :, 0:tiles * P], ps_p[:, k, 0:tiles * P]).then_inc(xh_ready, 1)

                def logits_out(g, tiles):
                    act.wait_ge(logitT_done, g + 1)
                    nc.scalar.copy(eight_rows[:, 0:tiles * P], ps_p[0:NX, 0, 0:tiles * P]).then_inc(logitT_ready, 1)

                def exponential(g, tiles):
                    act.wait_ge(gap_ready, g + 1)
                    nc.scalar.activation(wts[:, 1, 0:tiles], gap[:, 0:tiles], ACT.Exp).then_inc(e_ready, 1)

                def comb_out(g, tiles):
                    act.wait_ge(combT_done, g + 1)
                    nc.scalar.copy(eight_rows[:, 0:tiles * P], ps_p[0:NX, 0, 0:tiles * P]).then_inc(combT_ready, 1)

                halves(0, GT)

                def w2_high(q, u, i):
                    act.wait_ge(raw_in[u], i * 16 + 16)
                    nc.scalar.copy(piece(w2h, q), raw(u)).then_inc(raw_hi, 1)

                w2_loop(act, 0, w2_high)
                high_parts(0, GT)
                w2_loop(act, 1, w2_high)
                logits_out(0, GT)
                exponential(0, GT)
                comb_out(0, GT)

                def run(g, tiles, tiles_next, sums_before):
                    def hidden(e):
                        act.wait_ge(y_done, sums_before + (YC + (e - 1) * tiles if e else 1))
                        for k in range(KH):
                            n = e * KH + k
                            slot = (e % 2) * KH + k
                            act.wait_ge(h_done, g * HU + n + 1)
                            nc.scalar.activation(hh[:, slot, 0:tiles * P], ps_h[:, k, 0:tiles * P], ACT.Relu, bias=b1T[:, n:n + 1])
                            act.wait_ge(hT_ready, g * HU + n + 1)
                            nc.scalar.activation(h32[:, k % 2, 0:tiles * P], ps_h[:, k, 0:tiles * P], ACT.Relu,
                                                 bias=b1T[:, n:n + 1]).then_inc(h_out, 1)

                    hidden(0)
                    for e in range(NX):
                        if e + 1 < NX:
                            hidden(e + 1)
                        if not tiles_next:
                            continue
                        if e == 2:
                            halves(g + 1, tiles_next)
                        if e == 4:
                            high_parts(g + 1, tiles_next)
                        if e == 5:
                            logits_out(g + 1, tiles_next)
                            exponential(g + 1, tiles_next)
                        if e == 6:
                            comb_out(g + 1, tiles_next)

                all_groups(act, run)

            @block.vector
            def _(dve):
                dve.sem_inc(y_added, YB)
                dve.sem_inc(hT_ready, 2)
                dve.sem_inc(raw_used, RAW)

                def denominators(g, tiles):
                    dve.wait_ge(sums_in, 16 * g + 16)
                    nc.vector.tensor_scalar(rden[:, 0:tiles, :], sums[:, 0:tiles, D:ROW], TINY, None, ALU.max)
                    dve.drain()
                    nc.vector.reciprocal(rden[:, 0:tiles, :], rden[:, 0:tiles, :]).then_inc(rden_ready, 1)

                def normalise(rows_, into):
                    for j, r in enumerate(rows_):
                        nc.vector.bn_stats(stats[:, j, :], r)
                    dve.drain()
                    for j in range(len(rows_)):
                        nc.vector.bn_aggr(meanvar[:, j, :], stats[:, j, :])
                    dve.drain()
                    inverse_root(nc, meanvar[:, :, 1], roots, root_i, rstd[:])
                    for j, r in enumerate(rows_):
                        i = nc.vector.tensor_scalar(into[:, j, 0:D], r, meanvar[:, j, 0:1], rstd[:, j:j + 1], ALU.subtract, ALU.mult)
                    i.then_inc(norm_ready, 1)

                def first_norm(g, tiles):
                    dve.drain()
                    dve.wait_ge(o_ready, g + 1)
                    normalise([sums[:, j, 0:D] for j in range(tiles)], sums)

                def second_norm(g, tiles):
                    dve.drain()
                    dve.wait_ge(x1_ready, g + 1)
                    normalise([at(y, g, GT, j).rearrange("p a d -> p (a d)") for j in range(tiles)], tmp)

                def low_parts(g, tiles):
                    for k in range(KD):
                        dve.wait_ge(xh_ready, g * KD + k + 1)
                        nc.vector.tensor_tensor(at(xTl, g, KD, k)[:, :, 0:tiles * P], ps_p[:, k, 0:tiles * P].unsqueeze(1),
                                                at(xTh, g, KD, k)[:, :, 0:tiles * P].bitcast(F32), ALU.subtract).then_inc(xl_ready, 1)

                def choose(g, tiles):
                    lg, wk, rp = logit[:, 0:tiles, :], work[:, 0:tiles, :], ramp[:, 0:tiles, :]

                    def wide(v):
                        return v.unsqueeze(2).to_broadcast([P, tiles, NX])

                    dve.wait_ge(logit_done, g + 1)
                    nc.vector.tensor_tensor(lg, ps_p[:, 1, 0:tiles * NX].rearrange("p (t e) -> p t e", e=NX),
                                            gate_b[:, 0, :].unsqueeze(1).to_broadcast([P, tiles, NX]), ALU.add)
                    dve.drain()
                    for q in range(2):
                        nc.vector.tensor_reduce(top[:, q, 0:tiles], lg, AX.X, ALU.max)
                        dve.drain()
                        nc.vector.tensor_tensor(wk, lg, wide(top[:, q, 0:tiles]), ALU.is_equal)
                        dve.drain()
                        nc.vector.tensor_tensor(wk, wk, rp, ALU.mult)
                        dve.drain()
                        nc.vector.tensor_reduce(first[:, 0:tiles], wk, AX.X, ALU.min)
                        dve.drain()
                        nc.vector.tensor_tensor(pick[:, q, 0:tiles, :], rp, wide(first[:, 0:tiles]), ALU.is_equal)
                        dve.drain()
                        if q == 0:
                            nc.vector.tensor_scalar(wk, pick[:, 0, 0:tiles, :], -3e38, None, ALU.mult)
                            dve.drain()
                            nc.vector.tensor_tensor(lg, lg, wk, ALU.add)
                            dve.drain()
                    nc.vector.tensor_tensor(gap[:, 0:tiles], top[:, 1, 0:tiles], top[:, 0, 0:tiles], ALU.subtract).then_inc(gap_ready, 1)

                def combine(g, tiles):
                    def wide(v):
                        return v.unsqueeze(2).to_broadcast([P, tiles, NX])

                    dve.wait_ge(e_ready, g + 1)
                    nc.vector.tensor_scalar(wts[:, 0, 0:tiles], wts[:, 1, 0:tiles], 1.0, None, ALU.add)
                    dve.drain()
                    nc.vector.reciprocal(wts[:, 0, 0:tiles], wts[:, 0, 0:tiles])
                    dve.drain()
                    nc.vector.tensor_tensor(wts[:, 1, 0:tiles], wts[:, 1, 0:tiles], wts[:, 0, 0:tiles], ALU.mult)
                    dve.drain()
                    for q in range(2):
                        pk = pick[:, q, 0:tiles, :]
                        nc.vector.tensor_tensor(pk, pk, wide(wts[:, q, 0:tiles]), ALU.mult)
                    dve.drain()
                    nc.vector.tensor_tensor(comb_new[:, 0:tiles, :], pick[:, 0, 0:tiles, :], pick[:, 1, 0:tiles, :], ALU.add)
                    dve.drain()
                    nc.vector.tensor_copy(at(comb, g, GT, 0, tiles), comb_new[:, 0:tiles, :]).then_inc(comb_ready, 1)

                def add_b2(g, tiles):
                    dve.wait_ge(b2_done, g + 1)
                    for j in range(tiles):
                        yj = at(y, g, GT, j)
                        i = nc.vector.tensor_tensor(yj, yj, ps_p[:, j // 2, (j % 2) * D:(j % 2 + 1) * D].unsqueeze(1), ALU.add)
                    i.then_inc(b2_added, 1)

                nc.vector.memset(meanvar[:], 1.0)
                dve.drain()
                denominators(0, GT)
                first_norm(0, GT)
                dve.wait_ge(small_in, 16 * 5)
                nc.vector.tensor_copy(wgh[:], wg[:])
                nc.vector.tensor_tensor(gate_b[:, 0, :], gate_b[:, 0, :], gate_b[:, 1, :], ALU.add)
                dve.drain()
                nc.vector.tensor_tensor(wgl[:], wg[:], wgh[:].bitcast(F32), ALU.subtract)

                def w2_low(q, u, i):
                    dve.wait_ge(raw_hi, q + 1)
                    nc.vector.tensor_tensor(piece(w2l, q), raw(u), piece(w2h, q).bitcast(F32), ALU.subtract).then_inc(raw_used, 1)

                w2_loop(dve, 0, w2_low)
                dve.wait_ge(ramp_ready, 1)
                second_norm(0, GT)
                low_parts(0, GT)
                w2_loop(dve, 1, w2_low)
                dve.drain().then_inc(weights_ready, 1)
                choose(0, GT)
                combine(0, GT)
                add_b2(0, GT)

                def run(g, tiles, tiles_next, sums_before):
                    def split(e, k):
                        slot = (e % 2) * KH + k
                        dve.wait_ge(h_out, g * HU + (e + 1) * KH + k + 1)
                        nc.vector.tensor_tensor(hl[:, slot, 0:tiles * P], h32[:, k % 2, 0:tiles * P],
                                                hh[:, slot, 0:tiles * P].bitcast(F32), ALU.subtract).then_inc(hT_ready, 1)

                    def add_y(e, j):
                        dve.wait_ge(y_done, sums_before + e * tiles + j + 1 + YC)
                        yj = at(y, g, GT, j)
                        nc.vector.scalar_tensor_tensor(out=yj, in0=ps_y[:, (e * tiles + j) % YB, 0:D].unsqueeze(1),
                                                       scalar=at(comb, g, GT, j)[:, :, e:e + 1].rearrange("p a e -> p (a e)"), in1=yj,
                                                       op0=ALU.mult, op1=ALU.add).then_inc(y_added, 1)

                    dve.drain()
                    for k in range(KH):
                        split(0, k)
                    for e in range(NX):
                        if tiles == 1:
                            dve.drain()
                        for k in range(KH):
                            if k < tiles:
                                add_y(e, k)
                            if e + 1 < NX:
                                split(e + 1, k)
                        if not tiles_next:
                            continue
                        if e == 0:
                            denominators(g + 1, tiles_next)
                        if e == 1:
                            first_norm(g + 1, tiles_next)
                        if e == 3:
                            second_norm(g + 1, tiles_next)
                        if e == 4:
                            low_parts(g + 1, tiles_next)
                        if e == 5:
                            choose(g + 1, tiles_next)
                            combine(g + 1, tiles_next)
                        if e == 7:
                            add_b2(g + 1, tiles_next)

                all_groups(dve, run)

            @block.tensor
            def _(pe):
                pe.sem_inc(y_done, YC)
                pe.sem_inc(h_out, KH)
                pe.wait_ge(small_in, 16 * 5)
                nc.tensor.transpose(ps_y[:, 0, 0:NX * KH], b1_rows[:], ident[0:NX * KH, 0:NX * KH]).then_inc(b1T_done, 1)
                pe.wait_ge(b1T_ready, 1)

                def three(out_, ah, al, bh, bl, start, stop):
                    nc.tensor.matmul(out_, ah, bh, start=start, stop=False)
                    nc.tensor.matmul(out_, ah, bl, start=False, stop=False)
                    return nc.tensor.matmul(out_, al, bh, start=False, stop=stop)

                def xT(part, g, k, cols):
                    return at(part, g, KD, k)[:, :, 0:cols]

                def transpose_x(g, tiles):
                    pe.wait_ge(norm_ready, 2 * g + 2)
                    if not isinstance(g, int) or g > 0:
                        pe.wait_ge(b2_added, g)
                    for k in range(KD):
                        for j in range(tiles):
                            i = nc.tensor.transpose(ps_p[:, k, j * P:(j + 1) * P], tmp[:, j, k * P:(k + 1) * P], ident[:])
                    i.then_inc(xT_done, 1)

                def gate(g, tiles):
                    pe.wait_ge(xl_ready, g * KD + KD)
                    for k in range(KD):
                        i = three(ps_p[0:NX, 0, 0:tiles * P], wgh[:, k, :], wgl[:, k, :], xT(xTh, g, k, tiles * P), xT(xTl, g, k, tiles * P),
                                  k == 0, k == KD - 1)
                    i.then_inc(logitT_done, 1)

                def gate_back(g, tiles):
                    hold(pe, logitT_ready, g + 1, pe_passed)
                    for j in range(tiles):
                        i = nc.tensor.transpose(ps_p[:, 1, j * NX:(j + 1) * NX], eight_rows[:, j * P:(j + 1) * P], ident[0:NX, 0:NX])
                    i.then_inc(logit_done, 1)

                def transpose_comb(g, tiles):
                    pe.wait_ge(comb_ready, g + 1)
                    for j in range(tiles):
                        i = nc.tensor.transpose(ps_p[0:NX, 0, j * P:(j + 1) * P], comb_new[:, j, :], ident[:])
                    i.then_inc(combT_done, 1)

                def times_b2(g, tiles):
                    pe.wait_ge(combT_ready, g + 1)
                    for j in range(tiles):
                        i = nc.tensor.matmul(ps_p[:, j // 2, (j % 2) * D:(j % 2 + 1) * D], eight_rows[:, j * P:(j + 1) * P], b2_sb[:], start=True, stop=True)
                    i.then_inc(b2_done, 1)

                transpose_x(0, GT)
                gate(0, GT)
                gate_back(0, GT)
                transpose_comb(0, GT)
                times_b2(0, GT)

                def run(g, tiles, tiles_next, sums_before):
                    def first_layer(e):
                        for m in range(KH):
                            n = e * KH + m
                            pe.wait_ge(h_out, g * HU + n + 1)
                            for k in range(KD):
                                i = three(ps_h[:, m, 0:tiles * P], w1h[:, e * KD + k, m * P:(m + 1) * P], w1l[:, e * KD + k, m * P:(m + 1) * P],
                                          xT(xTh, g, k, tiles * P), xT(xTl, g, k, tiles * P), k == 0, k == KD - 1)
                            i.then_inc(h_done, 1)

                    def second_layer(e):
                        for j in range(tiles):
                            pe.wait_ge(y_added, sums_before + e * tiles + j + 1)
                            for k in range(KH):
                                if j == 0:
                                    pe.wait_ge(hT_ready, g * HU + e * KH + k + 3)
                                slot = (e % 2) * KH + k
                                i = three(ps_y[:, (e * tiles + j) % YB, 0:D], hh[:, slot, j * P:(j + 1) * P], hl[:, slot, j * P:(j + 1) * P],
                                          w2h[:, e * KH + k, :], w2l[:, e * KH + k, :], k == 0, k == KH - 1)
                            i.then_inc(y_done, 1)

                    first_layer(0)
                    if not isinstance(g, int):
                        pe.wait_ge(weights_ready, 1)
                    for e in range(NX):
                        if e + 1 < NX:
                            first_layer(e + 1)
                        if tiles_next and e == 5:
                            gate(g + 1, tiles_next)
                        second_layer(e)
                        if tiles_next and e == 4:
                            transpose_x(g + 1, tiles_next)
                        if tiles_next and e == 5:
                            gate_back(g + 1, tiles_next)
                        if tiles_next and e == 6:
                            transpose_comb(g + 1, tiles_next)
                        if tiles_next and e == 7:
                            times_b2(g + 1, tiles_next)

                all_groups(pe, run)


def kernel(**inputs):
    import concourse.bacc as bacc
    from concourse.bass_utils import run_bass_kernel_spmd

    a = {k: np.ascontiguousarray(v) for k, v in inputs.items()}
    x = np.zeros((NP_, D), np.float32)
    x[:N] = a["x"]
    src = np.zeros(EP, np.int32)
    src[:E] = a["src"]
    dst = np.full(EP, PAD_NODE, np.int32)
    dst[:E] = a["dst"]
    g = {k[len("L0_gnn_"):]: v for k, v in a.items() if k.startswith("L0_gnn_")}
    f = {k[len("L0_ffn_"):]: v for k, v in a.items() if k.startswith("L0_ffn_")}
    arrays = {
        "in_x": x,
        "in_src_idx": np.ascontiguousarray(src.reshape(NSUP, ET, P).transpose(0, 2, 1)),
        "in_dst_part": np.ascontiguousarray(dst.reshape(NSUP * ET, P).T),
        "in_dst_row": dst.reshape(NSUP, SUP),
        "in_W_src": g["W_src"], "in_W_dst": g["W_dst"],
        "in_att_src": g["att_src"].reshape(D), "in_att_dst": g["att_dst"].reshape(D),
        "in_bias": g["bias"], "in_ln_gamma": g["ln_gamma"], "in_ln_beta": g["ln_beta"], "in_prelu_w": g["prelu_w"],
        "in_Wg": f["Wg"], "in_bg": f["bg"], "in_gbias": f["bias"],
        "in_W1": f["W1"], "in_b1": f["b1"], "in_W2": f["W2"], "in_b2": f["b2"],
    }
    nc = bacc.Bacc("TRN2", target_bir_lowering=False, num_devices=1)
    args = [nc.dram_tensor(k, v.shape, mybir.dt.from_np(v.dtype), kind="ExternalInput").ap() for k, v in arrays.items()]
    args.append(nc.dram_tensor("out_x", (NP_, D), F32, kind="ExternalOutput").ap())
    build_program(nc, *args)
    r = run_bass_kernel_spmd(nc, [arrays], core_ids=[0])
    return r.results[0]["out_x"][:N]
```
